# Optimizing a Trainium2 kernel written in Bass

```python
import numpy as np
import jax
import jax.numpy as jnp

def _softmax(x, axis=-1):
    return jax.nn.softmax(x, axis=axis)

def _gelu(x):
    return jax.nn.gelu(x, approximate=True)

def _silu(x):
    return jax.nn.silu(x)

def _sigmoid(x):
    return jax.nn.sigmoid(x)

def _layernorm(x, axis=-1, eps=1e-05):
    m = jnp.mean(x, axis=axis, keepdims=True)
    v = jnp.var(x, axis=axis, keepdims=True)
    return (x - m) / jnp.sqrt(v + eps)

def _scatter_add(tgt, idx, src, axis=0):
    return tgt.at[idx].add(src)

def _segment_sum(src, seg, n):
    return jax.ops.segment_sum(src, seg, n)
kernel_name = 'mk_recurrent_d1_jaxref_r4_4bf4fc'

def setup_inputs(seed: int=0):
    np.random.seed(seed)
    _w = jnp.asarray

    def _L0_attn_setup():
        import jax, jax.numpy as jnp
        import numpy as np
        EPS = 1.1920929e-07

        def _rms(x):
            return x * jax.lax.rsqrt(jnp.mean(x * x, axis=-1, keepdims=True) + EPS)
        key = jax.random.key(seed)
        k0, k1, k2, k3 = jax.random.split(key, 4)
        B, S, D, DFF = (4, 512, 512, 2048)
        x = jax.random.normal(k0, (B, S, D), dtype=jnp.float32)
        w_qkv = jax.random.normal(k1, (3 * D, D), dtype=jnp.float32) * 0.02
        w_swiglu = jax.random.normal(k2, (2 * DFF, D), dtype=jnp.float32) * 0.02
        w_out = jax.random.normal(k3, (D, DFF), dtype=jnp.float32) * 0.02
        return {'x': x, 'w_qkv': w_qkv, 'w_swiglu': w_swiglu, 'w_out': w_out}
    _L0_attn_in = _L0_attn_setup()

    def _L0_ffn_setup():
        import jax, jax.numpy as jnp
        import numpy as np
        D_MODEL = 512
        D_EXPERT = 2048
        EPS = 1e-08

        def ternary_quant(w):
            scale = jnp.mean(jnp.abs(w)) + EPS
            q = jnp.clip(jnp.round(w / scale), -1.0, 1.0) * scale
            return w + jax.lax.stop_gradient(q - w)
        key = jax.random.key(seed)
        k_x, k_up, k_gate, k_down = jax.random.split(key, 4)
        std_in = 1.0 / np.sqrt(D_MODEL)
        std_exp = 1.0 / np.sqrt(D_EXPERT)
        return {'x': jax.random.normal(k_x, (4, 512, D_MODEL), dtype=jnp.float32), 'W_up': jax.random.normal(k_up, (D_EXPERT, D_MODEL), dtype=jnp.float32) * std_in, 'W_gate': jax.random.normal(k_gate, (D_EXPERT, D_MODEL), dtype=jnp.float32) * std_in, 'W_down': jax.random.normal(k_down, (D_MODEL, D_EXPERT), dtype=jnp.float32) * std_exp}
    _L0_ffn_in = _L0_ffn_setup()
    _d = {'L0_attn_x': _L0_attn_in['x'], 'L0_attn_w_qkv': _L0_attn_in['w_qkv'], 'L0_attn_w_swiglu': _L0_attn_in['w_swiglu'], 'L0_attn_w_out': _L0_attn_in['w_out'], 'L0_ffn_W_up': _L0_ffn_in['W_up'], 'L0_ffn_W_gate': _L0_ffn_in['W_gate'], 'L0_ffn_W_down': _L0_ffn_in['W_down']}
    _x0 = _d['L0_attn_x']
    _d['L0_attn_x'] = jax.random.normal(jax.random.fold_in(jax.random.key(seed), 1), (4, 1024, 512), dtype=_x0.dtype)
    del _x0
    return _d

def reference(L0_attn_x, L0_attn_w_qkv, L0_attn_w_swiglu, L0_attn_w_out, L0_ffn_W_up, L0_ffn_W_gate, L0_ffn_W_down):

    def _L0_attn_ref(x, w_qkv, w_swiglu, w_out):
        import jax, jax.numpy as jnp
        import numpy as np
        EPS = 1.1920929e-07

        def _rms(x):
            return x * jax.lax.rsqrt(jnp.mean(x * x, axis=-1, keepdims=True) + EPS)
        qkv = _rms(x) @ w_qkv.T
        q, k, v = jnp.split(qkv, 3, axis=-1)
        q = _rms(q)
        k = _rms(k)
        w = jnp.exp(k)
        kv_cum = jnp.cumsum(w * v, axis=1)
        w_cum = jnp.cumsum(w, axis=1)
        y = jax.nn.sigmoid(q) * (kv_cum / (w_cum + 1e-06))
        uv = y @ w_swiglu.T
        u, g = jnp.split(uv, 2, axis=-1)
        return x + u * jax.nn.silu(g) @ w_out.T

    def _L0_ffn_ref(x, W_up, W_gate, W_down):
        import jax, jax.numpy as jnp
        import numpy as np
        D_MODEL = 512
        D_EXPERT = 2048
        EPS = 1e-08

        def ternary_quant(w):
            scale = jnp.mean(jnp.abs(w)) + EPS
            q = jnp.clip(jnp.round(w / scale), -1.0, 1.0) * scale
            return w + jax.lax.stop_gradient(q - w)
        wu = ternary_quant(W_up)
        wg = ternary_quant(W_gate)
        wd = ternary_quant(W_down)
        up = jnp.einsum('bsd,ed->bse', x, wu)
        gate = jnp.einsum('bsd,ed->bse', x, wg)
        hidden = jax.nn.silu(up) * gate
        return jnp.einsum('bse,de->bsd', hidden, wd)
    x = L0_attn_x
    xn = _layernorm(x, axis=-1)
    s = _L0_attn_ref(xn, L0_attn_w_qkv, L0_attn_w_swiglu, L0_attn_w_out)
    g = _silu(_L0_ffn_ref(xn, L0_ffn_W_up, L0_ffn_W_gate, L0_ffn_W_down))
    x = x + s * g
    return x

_drawn_inputs = setup_inputs


def setup_inputs(seed=0):
    import zlib

    import numpy as np

    out = dict(_drawn_inputs(seed))
    spreads = {}
    factors = {'L0_attn_w_qkv': 8.0, 'L0_attn_w_swiglu': 8.0, 'L0_attn_w_out': 8.0}
    for name, (base, spread) in spreads.items():
        noise = np.random.default_rng([zlib.crc32(name.encode()), seed]).standard_normal(out[name].shape)
        drawn = base * np.exp(spread * noise) if base else spread * noise
        out[name] = jnp.asarray(drawn.astype(out[name].dtype))
    for name, factor in factors.items():
        out[name] = (out[name] * factor).astype(out[name].dtype)
    return out
```

```python
from contextlib import ExitStack

import concourse.bass as bass
from concourse import mybir

F32 = mybir.dt.float32
F32R = mybir.dt.float32r
F16 = mybir.dt.float16
U32 = mybir.dt.uint32
ALU = mybir.AluOpType
ACT = mybir.ActivationFunctionType
AX = mybir.AxisListType
RMAX = bass.bass_isa.ReduceOp.max

P = 128
B, S, D = 4, 1024, 512
E = 2048
T = 512
HALVES = S // T
CHUNKS = B * HALVES
KT = D // P
NJ = E // P
M3 = 3 * KT
LN_EPS = 1e-5
RMS_EPS = 1.1920929e-07
QUANT_EPS = 1e-8
DEN_EPS = 1e-6
LAG = 2
GRAN = 256

XS = 2.0 ** 10
HS = 2.0 ** -13
WTOP = 2.0 ** 14

QKV_ORDER = list(range(KT, 2 * KT)) + list(range(0, KT)) + list(range(2 * KT, 3 * KT))
K0, Q0, V0 = 0, KT, 2 * KT


class Signals:

    def __init__(self, nc, ctx, per_chunk, prefix=""):
        self.per = per_chunk
        self.sem = {n: ctx.enter_context(nc.semaphore(prefix + n)) for n in per_chunk}

    def __getitem__(self, name):
        return self.sem[name]

    def at(self, name, c, k):
        return c * self.per[name] + k

    def await_(self, eng, name, c, k):
        v = self.at(name, c, k)
        if isinstance(v, int) and v <= 0:
            return
        eng.wait_ge(self.sem[name], v)


def phase_a(nc, x_d, wqkv_d, ternary_d, xn_d, y_d, g_d):
    with ExitStack() as ctx:
        def sb(name, shape, dt):
            return ctx.enter_context(nc.sbuf_tensor("a_" + name, shape, dt))

        def pb(name):
            return ctx.enter_context(nc.psum_tensor("a_" + name, [P, T], F32))

        def sem(name):
            return ctx.enter_context(nc.semaphore("a_" + name))

        wq_hi = sb("wq_hi", [P, M3, KT, P], F16)
        wq_lo = sb("wq_lo", [P, M3, KT, P], F16)
        tern = [sb(n, [P, NJ * KT * P], F16) for n in ("tern_up", "tern_gate", "tern_down")]
        x = sb("x", [P, KT, T], F32)
        xh = sb("xh", [P, 2, KT, T], F16)
        xl = sb("xl", [P, 2, KT, T], F16)
        kqv = sb("kqv", [P, M3, T], F32)
        sq = sb("sq", [P, KT, T], F32)
        add2 = sb("add2", [P, 2, T], F32)
        add1 = sb("add1", [P, T], F32)
        var2 = sb("var2", [P, 2, T], F32)
        inv2 = sb("inv2", [P, 2, T], F32)
        r_t = sb("r_t", [P, T], F32)
        m2 = sb("m2", [P, T], F32)
        kq_ms = sb("kq_ms", [P, 2, T], F32)
        s_act = sb("s_act", [P, 2, T], F32)
        h = sb("h", [P, 2, T], F32)
        hh = sb("hh", [P, 3, T], F16)
        hl = sb("hl", [P, 3, T], F16)
        g_out = sb("g_out", [P, KT, T], F32)
        RING = 4
        stage = sb("stage", [P, RING, 1024], F32)
        below = sb("below", [P, 2, 1024], F16)
        mean_w = sb("mean_w", [P, P], F32)
        count_w = sb("count_w", [P, P], F32)
        one_col = sb("one_col", [P, 1], F32)
        carry = sb("carry", [P, 2, KT], F32)
        absum = sb("absum", [P, 3, 8], F32)
        absum3 = sb("absum3", [P, 3], F32)
        absjunk = sb("absjunk", [P, 1024], F16)
        scale3 = sb("scale3", [P, 3], F32)
        half3 = sb("half3", [P, 3], F32)
        nhalf3 = sb("nhalf3", [P, 3], F32)
        c_up = sb("c_up", [P, 1], F32)
        inv_up = sb("inv_up", [P, 2], F32)
        c_ffn = sb("c_ffn", [P, 3], F32)
        wmax = sb("wmax", [P, 6], F32)
        wpow = sb("wpow", [P, 1], F32)
        s_w = sb("s_w", [P, 2], F32)
        c_w = sb("c_w", [P, 1], F32)

        ring = [pb(f"ring{i}") for i in range(3)]
        acc = [pb(f"acc{i}") for i in range(KT)]
        stat = pb("stat")

        S_ = Signals(nc, ctx, {
            "x_loaded": 16, "xn_stored": 16, "y_stored": 16, "g_stored": 16,
            "fold_half": 4, "fold_done": 4, "stat_mm": 4, "stat_read": 4, "sq_done": 3,
            "centred": 1, "var_root": 1, "inv_x": 2 * T // GRAN, "norms": 3, "xh_done": 1, "xl_done": 1,
            "qkv_mm": M3, "qkv_read": M3, "kq_root": 1, "inv_kq": 2 * T // GRAN, "kq_scaled": 2 * KT,
            "exped": 2, "wv_done": KT, "summed": 2 * KT + 2, "den_done": 1, "inv_den": KT * T // GRAN,
            "y_done": KT, "u_mm": NJ, "g_mm": NJ, "s_done": NJ, "h_done": NJ, "hh_done": NJ, "hl_done": NJ,
            "down_done": NJ, "g_act": KT,
        }, "a_")
        wq_in = [sem(f"wq_in{i}") for i in range(4)]
        stage_in = [sem(f"stage_in{i}") for i in range(RING)]
        stage_used = sem("stage_used")
        consts = sem("consts")
        wmax_s = sem("wmax")
        wscale = sem("wscale")
        wq_hi_s = sem("wq_hi")
        wq_lo_s = sem("wq_lo")
        absum_s = sem("absum")
        mean3_s = sem("mean3")
        scales_s = sem("scales")
        below_s = sem("below")
        tern_s = sem("tern")

        wq_raw = kqv
        wq_raw_f = wq_raw[:, :, :].rearrange("p a b -> p (a b)")
        wq_hi_f = wq_hi[:, :, :, :].rearrange("p a b c -> p (a b c)")
        wq_lo_f = wq_lo[:, :, :, :].rearrange("p a b c -> p (a b c)")
        WQ = M3 * D // 4
        up = tern[0][:, :].rearrange("p (j k m) -> p j k m", j=NJ, k=KT)
        gate = tern[1][:, :].rearrange("p (j k m) -> p j k m", j=NJ, k=KT)
        down = tern[2][:, :].rearrange("p (j n) -> p j n", j=NJ)
        pieces = [(m, g) for m in range(3) for g in range(8)] + [(m, g) for g in range(8) for m in range(3)]
        NSUM = 24

        def wide(t):
            return t.unsqueeze(1).to_broadcast([P, KT, T])

        block = ctx.enter_context(nc.Block())

        @block.sync
        def _(sp):
            sp.dma_start(x[:, :, :], x_d[0]).then_inc(S_["x_loaded"], 16)
            for i in range(4):
                sp.dma_start(wq_raw_f[:, i * WQ:(i + 1) * WQ], wqkv_d[i]).then_inc(wq_in[i], 16)
            for n, (m, g) in enumerate(pieces):
                if n >= RING:
                    sp.wait_ge(stage_used, n - RING + 1)
                sp.dma_start(stage[:, n % RING, :], ternary_d[m][g]).then_inc(stage_in[n % RING], 16)

            def chunk(c, nxt):
                S_.await_(sp, "norms", c, 3)
                sp.dma_start(xn_d[bass.ds(c, 1)].rearrange("c p k t -> p (c k) t"), x[:, :, :])\
                    .then_inc(S_["xn_stored"], 16)
                S_.await_(sp, "xh_done", c, 1)
                S_.await_(sp, "xl_done", c, 1)
                S_.await_(sp, "xn_stored", c, 16)
                sp.dma_start(x[:, :, :], x_d[bass.ds(nxt, 1)].rearrange("c p k t -> p (c k) t"))\
                    .then_inc(S_["x_loaded"], 16)
                S_.await_(sp, "y_done", c, KT)
                sp.dma_start(y_d[bass.ds(c, 1)].rearrange("c p k t -> p (c k) t"), kqv[:, V0:V0 + KT, :])\
                    .then_inc(S_["y_stored"], 16)
                S_.await_(sp, "g_act", c, KT)
                sp.dma_start(g_d[bass.ds(c, 1)].rearrange("c p k t -> p (c k) t"), g_out[:, :, :])\
                    .then_inc(S_["g_stored"], 16)

            for half in range(HALVES):
                chunk(half, half + 1)
            with sp.Fori(1, B) as b:
                for half in range(HALVES):
                    c = b * HALVES + half
                    chunk(c, c + 1 if half + 1 < HALVES else (c + 1) % CHUNKS)
            sp.wait_ge(S_["x_loaded"], 16 * (CHUNKS + 1))
            for name in ("xn_stored", "y_stored", "g_stored"):
                sp.wait_ge(S_[name], 16 * CHUNKS)

        @block.gpsimd
        def _(pool):
            pool.memset(mean_w[:, :], 1.0 / D).then_inc(consts, 1)
            pool.memset(count_w[:, :], 1.0 / (E * D)).then_inc(consts, 1)
            pool.memset(one_col[:, :], 1.0).then_inc(consts, 1)

            def fold(c, k, src):
                S_.await_(pool, "stat_mm", c, k - 1)
                S_.await_(pool, "fold_done", c, k - 1)
                pool.tensor_tensor(add2[:, :, :], src[:, 0:2, :], src[:, 2:4, :], ALU.add)\
                    .then_inc(S_["fold_half"], 1)
                S_.await_(pool, "fold_half", c, k)
                pool.tensor_tensor(add1[:, :], add2[:, 0, :], add2[:, 1, :], ALU.add)\
                    .then_inc(S_["fold_done"], 1)

            S_.await_(pool, "x_loaded", 0, 16)
            fold(0, 1, x)
            pool.wait_ge(wmax_s, 5)
            pool.partition_all_reduce(wmax[:, 5:6], wmax[:, 4:5], P, RMAX).then_inc(wmax_s, 1)
            S_.await_(pool, "sq_done", 0, 1)
            fold(0, 2, sq)

            def chunk(c):
                S_.await_(pool, "sq_done", c, 2)
                fold(c, 3, sq)
                S_.await_(pool, "sq_done", c, 3)
                fold(c, 4, sq)
                S_.await_(pool, "x_loaded", c + 1, 16)
                fold(c, 5, x)

                def scale_kq(t):
                    which = t // KT
                    S_.await_(pool, "inv_kq", c, (which + 1) * (T // GRAN))
                    pool.tensor_tensor(kqv[:, t, :], kqv[:, t, :], kq_ms[:, which, :], ALU.mult)\
                        .then_inc(S_["kq_scaled"], 1)

                def wv(t):
                    S_.await_(pool, "exped", c, 1)
                    pool.tensor_tensor(kqv[:, V0 + t, :], kqv[:, V0 + t, :], kqv[:, K0 + t, :], ALU.mult)\
                        .then_inc(S_["wv_done"], 1)

                def y(t):
                    S_.await_(pool, "inv_den", c, (t + 1) * (T // GRAN))
                    pool.tensor_tensor(kqv[:, V0 + t, :], kqv[:, V0 + t, :], kqv[:, Q0 + t, :], ALU.mult)\
                        .then_inc(S_["y_done"], 1)

                def var_fold():
                    S_.await_(pool, "sq_done", c, 4)
                    fold(c, 6, sq)

                jobs = {1: [(scale_kq, 0), (scale_kq, 1)], 2: [(scale_kq, 2), (scale_kq, 3)],
                        3: [(scale_kq, 4), (scale_kq, 5)], 4: [(scale_kq, 6), (scale_kq, 7)],
                        5: [(wv, 0), (wv, 1)], 6: [(wv, 2), (wv, 3)], 7: [(var_fold,)],
                        12: [(y, 0)], 13: [(y, 1)], 16: [(y, 2), (y, 3)]}
                for j in range(NJ + 1):
                    if j >= 1:
                        i = j - 1
                        S_.await_(pool, "hh_done", c, i + 1)
                        S_.await_(pool, "down_done", c, i - 2)
                        pool.tensor_tensor(hl[:, i % 3, :], h[:, i % 2, :], hh[:, i % 3, :], ALU.subtract)\
                            .then_inc(S_["hl_done"], 1)
                    for job in jobs.get(j, []):
                        job[0](*job[1:])

            pool.wait_ge(wq_lo_s, 4)
            for half in range(HALVES):
                chunk(half)
            with pool.Fori(1, B) as b:
                for half in range(HALVES):
                    chunk(b * HALVES + half)

        @block.scalar
        def _(act):
            def roots(c):
                S_.await_(act, "stat_read", c, 6)
                act.activation(var2[:, :, :], var2[:, :, :], ACT.Sqrt).then_inc(S_["var_root"], 1)

            def square_x(c, k):
                S_.await_(act, "centred", c + 1, 1)
                S_.await_(act, "fold_half", c, k)
                act.activation(sq[:, :, :], x[:, :, :], ACT.Square).then_inc(S_["sq_done"], 1)

            def high_x(c, slot):
                S_.await_(act, "norms", c + 1, 3)
                S_.await_(act, "g_mm", c, 0)
                act.activation(xh[:, slot, :, :], x[:, :, :], ACT.Copy, scale=XS).then_inc(S_["xh_done"], 1)

            S_.await_(act, "centred", 0, 1)
            act.activation(sq[:, :, :], x[:, :, :], ACT.Square).then_inc(S_["sq_done"], 1)
            act.wait_ge(wscale, 3)
            for i in range(4):
                act.activation(wq_hi_f[:, i * WQ:(i + 1) * WQ], wq_raw_f[:, i * WQ:(i + 1) * WQ], ACT.Copy,
                               scale=s_w[:, 0:1]).then_inc(wq_hi_s, 1)
            roots(-1)
            high_x(-1, 0)
            for n in range(NSUM):
                m, g = pieces[n]
                act.wait_ge(stage_in[n % RING], 16 * (n // RING + 1))
                if n >= 1:
                    act.wait_ge(stage_used, n)
                act.activation(absjunk[:, :], stage[:, n % RING, :], ACT.Abs,
                               accum_out=absum[:, m, g:g + 1]).then_inc(stage_used, 1)
            act.wait_ge(scales_s, 6)

            def chunk(c, half):
                S_.await_(act, "qkv_read", c, KT)
                S_.await_(act, "fold_half", c, 2)
                act.activation(sq[:, :, :], kqv[:, K0:K0 + KT, :], ACT.Square).then_inc(S_["sq_done"], 1)
                S_.await_(act, "qkv_read", c, 2 * KT)
                S_.await_(act, "fold_half", c, 3)
                act.activation(sq[:, :, :], kqv[:, Q0:Q0 + KT, :], ACT.Square).then_inc(S_["sq_done"], 1)
                S_.await_(act, "stat_read", c, 4)
                act.activation(kq_ms[:, :, :], kq_ms[:, :, :], ACT.Sqrt).then_inc(S_["kq_root"], 1)

                def exp_kq():
                    S_.await_(act, "kq_scaled", c, KT)
                    act.activation(kqv[:, K0:K0 + KT, :], kqv[:, K0:K0 + KT, :], ACT.Exp)\
                        .then_inc(S_["exped"], 1)
                    S_.await_(act, "kq_scaled", c, 2 * KT)
                    act.activation(kqv[:, Q0:Q0 + KT, :], kqv[:, Q0:Q0 + KT, :], ACT.Exp, scale=-1.0)\
                        .then_inc(S_["exped"], 1)

                jobs = {3: (square_x, c, 4), 5: (exp_kq,), 9: (roots, c), 14: (high_x, c, 1 - half)}
                for j in range(NJ + 1):
                    if j < NJ:
                        S_.await_(act, "u_mm", c, j + 1)
                        S_.await_(act, "h_done", c, j - 1)
                        act.activation(s_act[:, j % 2, :], ring[2 * j % 3][:, :], ACT.Silu, scale=c_up[:, 0:1])\
                            .then_inc(S_["s_done"], 1)
                    if j >= 1:
                        i = j - 1
                        S_.await_(act, "h_done", c, i + 1)
                        S_.await_(act, "down_done", c, i - 2)
                        act.activation(hh[:, i % 3, :], h[:, i % 2, :], ACT.Copy).then_inc(S_["hh_done"], 1)
                    if j in jobs:
                        jobs[j][0](*jobs[j][1:])
                S_.await_(act, "down_done", c, NJ)
                S_.await_(act, "g_stored", c, 0)
                for t in range(KT):
                    act.activation(g_out[:, t, :], acc[t][:, :], ACT.Silu, scale=c_ffn[:, 2:3])\
                        .then_inc(S_["g_act"], 1)

            for half in range(HALVES):
                chunk(half, half)
            with act.Fori(1, B) as b:
                for half in range(HALVES):
                    chunk(b * HALVES + half, half)

        @block.vector
        def _(dve):
            PER_T = T // GRAN

            def centre(c):
                S_.await_(dve, "stat_mm", c, 5)
                S_.await_(dve, "x_loaded", c + 1, 16)
                dve.tensor_tensor(x[:, :, :], x[:, :, :], wide(stat[:, :]), ALU.subtract)\
                    .then_inc(S_["centred"], 1)
                S_.await_(dve, "centred", c + 1, 1)
                dve.sem_inc(S_["stat_read"], 1)

            def variances(c):
                S_.await_(dve, "stat_mm", c, 6)
                S_.await_(dve, "norms", c + 1, 0)
                dve.tensor_scalar(var2[:, 0, :], stat[:, :], LN_EPS, None, ALU.add)
                dve.tensor_scalar(var2[:, 1, :], stat[:, :], 1.0 + RMS_EPS, RMS_EPS * LN_EPS,
                                  ALU.mult, ALU.add).then_inc(S_["stat_read"], 1)

            def invert_x(c, g):
                i, o = g // PER_T, g % PER_T * GRAN
                S_.await_(dve, "var_root", c + 1, 1)
                dve.reciprocal(inv2[:, i, o:o + GRAN], var2[:, i, o:o + GRAN]).then_inc(S_["inv_x"], 1)

            def norms(c):
                S_.await_(dve, "inv_x", c + 1, 2 * PER_T)
                dve.tensor_tensor(r_t[:, :], var2[:, 0, :], inv2[:, 1, :], ALU.mult)
                dve.tensor_tensor(m2[:, :], var2[:, 1, :], inv2[:, 0, :], ALU.mult).then_inc(S_["norms"], 1)
                S_.await_(dve, "norms", c + 1, 1)
                dve.tensor_tensor(m2[:, :], m2[:, :], m2[:, :], ALU.mult).then_inc(S_["norms"], 1)
                dve.tensor_tensor(x[:, :, :], x[:, :, :], wide(inv2[:, 0, :]), ALU.mult)\
                    .then_inc(S_["norms"], 1)

            def low_x(c, slot):
                S_.await_(dve, "norms", c + 1, 3)
                S_.await_(dve, "xh_done", c + 1, 1)
                dve.scalar_tensor_tensor(xl[:, slot, :, :], x[:, :, :], XS, xh[:, slot, :, :],
                                         ALU.mult, ALU.subtract).then_inc(S_["xl_done"], 1)

            centre(-1)
            for i in range(4):
                dve.wait_ge(wq_in[i], 16)
                dve.tensor_reduce(wmax[:, i:i + 1], wq_raw_f[:, i * WQ:(i + 1) * WQ], AX.X, ALU.max,
                                  apply_absolute_value=True).then_inc(wmax_s, 1)
            dve.wait_ge(wmax_s, 4)
            dve.tensor_reduce(wmax[:, 4:5], wmax[:, 0:4], AX.X, ALU.max).then_inc(wmax_s, 1)
            dve.wait_ge(wmax_s, 6)
            dve.tensor_scalar(wpow[:, :], wmax[:, 5:6], 1e-30, None, ALU.max).then_inc(wscale, 1)
            dve.wait_ge(wscale, 1)
            dve.tensor_scalar(c_w[:, :].bitcast(U32), wpow[:, :].bitcast(U32), 0x7F800000, None,
                              ALU.bitwise_and).then_inc(wscale, 1)
            dve.wait_ge(wscale, 2)
            dve.reciprocal(s_w[:, 1:2], c_w[:, :]).then_inc(wq_lo_s, 1)
            dve.wait_ge(wq_lo_s, 1)
            dve.tensor_scalar(s_w[:, 0:1], s_w[:, 1:2], WTOP, None, ALU.mult).then_inc(wscale, 1)
            dve.tensor_scalar(c_w[:, :], c_w[:, :], 1.0 / (WTOP * XS), None, ALU.mult).then_inc(wscale, 1)
            dve.wait_ge(wscale, 4)
            for i in range(4):
                dve.wait_ge(wq_hi_s, i + 1)
                dve.scalar_tensor_tensor(wq_lo_f[:, i * WQ:(i + 1) * WQ], wq_raw_f[:, i * WQ:(i + 1) * WQ],
                                         s_w[:, 0:1], wq_hi_f[:, i * WQ:(i + 1) * WQ],
                                         ALU.mult, ALU.subtract).then_inc(wq_lo_s, 1)
                if i == 0:
                    variances(-1)
                if i == 1:
                    for g in range(2 * PER_T):
                        invert_x(-1, g)
                    norms(-1)
            low_x(-1, 0)
            dve.wait_ge(stage_used, NSUM)
            dve.tensor_reduce(absum3[:, :], absum[:, :, :], AX.X, ALU.add).then_inc(absum_s, 1)
            dve.wait_ge(mean3_s, 1)
            dve.tensor_scalar(scale3[:, :], stat[:, 0:3], QUANT_EPS, None, ALU.add).then_inc(absum_s, 1)
            dve.wait_ge(absum_s, 2)
            dve.tensor_scalar(half3[:, :], scale3[:, :], 0.5, None, ALU.mult).then_inc(scales_s, 1)
            dve.tensor_scalar(nhalf3[:, :], scale3[:, :], -0.5, None, ALU.mult).then_inc(scales_s, 1)
            dve.tensor_scalar(c_up[:, :], scale3[:, 0:1], 1.0 / XS, None, ALU.mult).then_inc(scales_s, 1)
            dve.reciprocal(inv_up[:, 0:1], scale3[:, 0:1]).then_inc(absum_s, 1)
            dve.tensor_tensor(c_ffn[:, 0:1], scale3[:, 0:1], scale3[:, 1:2], ALU.mult).then_inc(absum_s, 1)
            dve.wait_ge(absum_s, 4)
            dve.tensor_scalar(inv_up[:, 1:2], inv_up[:, 0:1], HS, None, ALU.mult).then_inc(scales_s, 1)
            dve.tensor_tensor(c_ffn[:, 1:2], c_ffn[:, 0:1], scale3[:, 2:3], ALU.mult).then_inc(scales_s, 1)
            dve.wait_ge(scales_s, 5)
            dve.tensor_scalar(c_ffn[:, 2:3], c_ffn[:, 1:2], 1.0 / (HS * XS), None, ALU.mult).then_inc(scales_s, 1)
            dve.wait_ge(scales_s, 6)
            for n in range(NSUM, len(pieces)):
                m, g = pieces[n]
                dve.wait_ge(stage_in[n % RING], 16 * (n // RING + 1))
                i = n - NSUM
                if i >= 2:
                    dve.wait_ge(tern_s, i - 1)
                dve.tensor_scalar(below[:, i % 2, :], stage[:, n % RING, :], nhalf3[:, m:m + 1], None, ALU.is_lt)\
                    .then_inc(below_s, 1)
                dve.wait_ge(below_s, i + 1)
                dve.scalar_tensor_tensor(tern[m][:, g * 1024:(g + 1) * 1024], stage[:, n % RING, :],
                                         half3[:, m:m + 1], below[:, i % 2, :], ALU.is_gt, ALU.subtract)\
                    .then_inc(tern_s, 1)
                dve.wait_ge(tern_s, i + 1)
                dve.sem_inc(stage_used, 1)

            def chunk(c, half):
                def read_qkv(n):
                    S_.await_(dve, "qkv_mm", c, n + 1)
                    if n < 2 * KT:
                        if n >= KT:
                            S_.await_(dve, "y_done", c, 0)
                        dve.tensor_scalar(kqv[:, n, :], ring[n % 3][:, :], c_w[:, 0:1], None, ALU.mult)\
                            .then_inc(S_["qkv_read"], 1)
                    else:
                        S_.await_(dve, "y_stored", c, 0)
                        dve.scalar_tensor_tensor(kqv[:, n, :], ring[n % 3][:, :], c_w[:, 0:1], r_t[:, :],
                                                 ALU.mult, ALU.mult).then_inc(S_["qkv_read"], 1)

                def mean_square(which):
                    S_.await_(dve, "stat_mm", c, 3 + which)
                    dve.scalar_tensor_tensor(kq_ms[:, which, :], m2[:, :], RMS_EPS, stat[:, :],
                                             ALU.mult, ALU.add).then_inc(S_["stat_read"], 1)

                S_.await_(dve, "den_done", c, 0)
                for n in range(M3):
                    read_qkv(n)
                    if n == 2 * KT:
                        mean_square(0)
                mean_square(1)

                def invert_kq(g):
                    i, o = g // PER_T, g % PER_T * GRAN
                    S_.await_(dve, "kq_root", c, 1)
                    dve.reciprocal(kq_ms[:, i, o:o + GRAN], kq_ms[:, i, o:o + GRAN]).then_inc(S_["inv_kq"], 1)

                def running_sum(n):
                    which, t = n // KT, n % KT
                    tile = (K0 if which == 0 else V0) + t
                    if which == 0:
                        S_.await_(dve, "wv_done", c, KT)
                    start = carry[:, which, t:t + 1] if half else (DEN_EPS if which == 0 else 0.0)
                    dve.tensor_tensor_scan(kqv[:, tile, :], one_col[:, 0:1].to_broadcast([P, T]),
                                           kqv[:, tile, :], start, ALU.mult, ALU.add)\
                        .then_inc(S_["summed"], 1)

                def keep_ends():
                    S_.await_(dve, "summed", c, 2 * KT)
                    for which, tile in ((0, K0), (1, V0)):
                        dve.tensor_copy(carry[:, which, :], kqv[:, tile:tile + KT, T - 1:T]
                                        .rearrange("p k o -> p (k o)")).then_inc(S_["summed"], 1)

                def denominators():
                    S_.await_(dve, "exped", c, 2)
                    S_.await_(dve, "summed", c, KT)
                    dve.scalar_tensor_tensor(kqv[:, Q0:Q0 + KT, :], kqv[:, Q0:Q0 + KT, :], 1.0,
                                             kqv[:, K0:K0 + KT, :], ALU.add, ALU.mult)\
                        .then_inc(S_["den_done"], 1)

                def invert_den(g):
                    t, o = Q0 + g // PER_T, g % PER_T * GRAN
                    S_.await_(dve, "den_done", c, 1)
                    S_.await_(dve, "summed", c, 2 * KT + 2)
                    dve.reciprocal(kqv[:, t, o:o + GRAN], kqv[:, t, o:o + GRAN]).then_inc(S_["inv_den"], 1)

                jobs = {0: [(invert_kq, 0), (invert_kq, 1)], 1: [(invert_kq, 2), (invert_kq, 3)],
                        2: [(centre, c)],
                        7: [(running_sum, 0), (running_sum, 1), (running_sum, 2)],
                        8: [(running_sum, 3), (running_sum, 4), (running_sum, 5)],
                        9: [(variances, c), (running_sum, 6), (running_sum, 7), (keep_ends,)],
                        10: [(denominators,), (invert_den, 0)],
                        11: [(invert_den, 1), (invert_den, 2)],
                        12: [(invert_den, 3), (invert_den, 4), ],
                        13: [(invert_x, c, 0), (invert_x, c, 1)],
                        14: [(invert_x, c, 2), (invert_x, c, 3), (norms, c)],
                        15: [(invert_den, 5), (invert_den, 6)],
                        16: [(low_x, c, 1 - half), (invert_den, 7)]}
                for j in range(NJ + 1):
                    if j < NJ:
                        S_.await_(dve, "s_done", c, j + 1)
                        S_.await_(dve, "g_mm", c, j + 1)
                        S_.await_(dve, "hl_done", c, j - 1)
                        S_.await_(dve, "hh_done", c, j - 1)
                        dve.scalar_tensor_tensor(h[:, j % 2, :], s_act[:, j % 2, :], inv_up[:, 1:2],
                                                 ring[(2 * j + 1) % 3][:, :], ALU.mult, ALU.mult)\
                            .then_inc(S_["h_done"], 1)
                    for job in jobs.get(j, []):
                        job[0](*job[1:])

            for half in range(HALVES):
                chunk(half, half)
            with dve.Fori(1, B) as b:
                for half in range(HALVES):
                    chunk(b * HALVES + half, half)

        @block.tensor
        def _(pe):
            def mean_over_features(c, k):
                S_.await_(pe, "fold_done", c, k)
                S_.await_(pe, "stat_read", c, k - 1)
                pe.matmul(stat[:, :], mean_w[:, :], add1[:, :], start=True, stop=True)\
                    .then_inc(S_["stat_mm"], 1)

            pe.wait_ge(consts, 3)
            mean_over_features(0, 1)
            mean_over_features(0, 2)
            pe.wait_ge(absum_s, 1)
            S_.await_(pe, "stat_read", 0, 2)
            pe.matmul(stat[:, 0:3], count_w[:, :], absum3[:, :], start=True, stop=True).then_inc(mean3_s, 1)
            pe.wait_ge(absum_s, 2)
            pe.wait_ge(wq_lo_s, 5)

            def chunk(c, half):
                S_.await_(pe, "xh_done", c, 1)
                S_.await_(pe, "xl_done", c, 1)
                for n, m in enumerate(QKV_ORDER):
                    if n >= 3:
                        S_.await_(pe, "qkv_read", c, n - 2)
                    elif n == 0:
                        S_.await_(pe, "s_done", c, 0)
                        S_.await_(pe, "h_done", c, 0)
                    i = 0
                    for k in range(KT):
                        for w, a in ((wq_hi, xh), (wq_hi, xl), (wq_lo, xh)):
                            last = pe.matmul(ring[n % 3][:, :], w[:, m, k, :], a[:, half, k, :],
                                             start=(i == 0), stop=(i == 3 * KT - 1))
                            i += 1
                    last.then_inc(S_["qkv_mm"], 1)
                    if n == 2 * KT:
                        mean_over_features(c, 3)
                mean_over_features(c, 4)

                def project(w, j, bank, done):
                    for i in range(2 * KT):
                        last = pe.matmul(bank[:, :], w[:, j, i // 2, :], (xh, xl)[i % 2][:, half, i // 2, :],
                                         start=(i == 0), stop=(i == 2 * KT - 1))
                    last.then_inc(S_[done], 1)

                for j in range(NJ + LAG):
                    if j < NJ:
                        for which in range(2):
                            m = 2 * j + which
                            if m < 3:
                                S_.await_(pe, "qkv_read", c, M3 - 2 + m)
                            elif (m - 3) % 2 == 0:
                                S_.await_(pe, "s_done", c, (m - 3) // 2 + 1)
                            else:
                                S_.await_(pe, "h_done", c, (m - 3) // 2 + 1)
                            project((up, gate)[which], j, ring[m % 3], ("u_mm", "g_mm")[which])
                    if j >= LAG:
                        i = j - LAG
                        S_.await_(pe, "hl_done", c, i + 1)
                        if i == 0:
                            S_.await_(pe, "g_act", c, 0)
                        for t in range(KT):
                            pe.matmul(acc[t][:, :], down[:, i, t * P:(t + 1) * P], hh[:, i % 3, :],
                                      start=(i == 0), stop=False)
                            last = pe.matmul(acc[t][:, :], down[:, i, t * P:(t + 1) * P], hl[:, i % 3, :],
                                             start=False, stop=(i == NJ - 1))
                        last.then_inc(S_["down_done"], 1)
                    if j == 1:
                        mean_over_features(c, 5)
                    if j == 8:
                        mean_over_features(c, 6)

            pe.wait_ge(tern_s, 24)
            for half in range(HALVES):
                chunk(half, half)
            with pe.Fori(1, B) as b:
                for half in range(HALVES):
                    chunk(b * HALVES + half, half)


def phase_b(nc, x_d, wswi_d, wout_d, xn_d, y_d, g_d, out_d):
    with ExitStack() as ctx:
        def sb(name, shape, dt):
            return ctx.enter_context(nc.sbuf_tensor("b_" + name, shape, dt))

        def pb(name):
            return ctx.enter_context(nc.psum_tensor("b_" + name, [P, T], F32))

        def sem(name):
            return ctx.enter_context(nc.semaphore("b_" + name))

        UNIT = 2 * KT * P
        swi = sb("swi", [P, NJ, UNIT], F32)
        wout = sb("wout", [P, NJ, D], F32)
        swi_hi = sb("swi_hi", [P, 2, UNIT], F32R)
        swi_lo = sb("swi_lo", [P, 2, UNIT], F32R)
        out_hi = sb("out_hi", [P, 2, D], F32R)
        out_lo = sb("out_lo", [P, 2, D], F32R)
        y = sb("y", [P, KT, T], F32)
        yh = sb("yh", [P, 2, KT, T], F32R)
        yl = sb("yl", [P, 2, KT, T], F32R)
        s_act = sb("s_act", [P, 2, T], F32)
        h = sb("h", [P, 2, T], F32)
        hh = sb("hh", [P, 3, T], F32R)
        hl = sb("hl", [P, 3, T], F32R)
        x = sb("x", [P, KT, T], F32)
        xn = sb("xn", [P, KT, T], F32)
        g = sb("g", [P, KT, T], F32)

        ring = [pb(f"ring{i}") for i in range(4)]
        acc = [pb(f"acc{i}") for i in range(KT)]

        S_ = Signals(nc, ctx, {
            "y_loaded": 16, "tail_loaded": 48, "out_stored": 16, "yh_done": 1, "yl_done": 1,
            "swi_hi": NJ, "swi_lo": NJ, "out_hi": NJ, "out_lo": NJ,
            "u_mm": NJ, "g_mm": NJ, "s_done": NJ, "h_done": NJ, "hh_done": NJ, "hl_done": NJ,
            "down_done": NJ, "acc_read": KT, "gated": 1, "out_ready": 1,
        }, "b_")
        swi_in = [sem(f"swi_in{j}") for j in range(NJ)]
        out_in = [sem(f"out_in{j}") for j in range(NJ)]

        block = ctx.enter_context(nc.Block())

        @block.sync
        def _(sp):
            sp.dma_start(y[:, :, :], y_d[0]).then_inc(S_["y_loaded"], 16)
            for j in range(NJ):
                sp.dma_start(swi[:, j, :], wswi_d[j]).then_inc(swi_in[j], 16)
                sp.dma_start(wout[:, j, :], wout_d[j]).then_inc(out_in[j], 16)

            def chunk(c, nxt):
                S_.await_(sp, "yh_done", c, 1)
                S_.await_(sp, "yl_done", c, 1)
                sp.dma_start(y[:, :, :], y_d[bass.ds(nxt, 1)].rearrange("c p k t -> p (c k) t"))\
                    .then_inc(S_["y_loaded"], 16)
                S_.await_(sp, "out_stored", c, 0)
                S_.await_(sp, "out_ready", c, 0)
                for dst, src in ((xn, xn_d), (g, g_d), (x, x_d)):
                    sp.dma_start(dst[:, :, :], src[bass.ds(c, 1)].rearrange("c p k t -> p (c k) t"))\
                        .then_inc(S_["tail_loaded"], 16)
                S_.await_(sp, "out_ready", c, 1)
                sp.dma_start(out_d[bass.ds(c, 1)].rearrange("c p k t -> p (c k) t"), xn[:, :, :])\
                    .then_inc(S_["out_stored"], 16)

            for half in range(HALVES):
                chunk(half, half + 1)
            with sp.Fori(1, B) as b:
                for half in range(HALVES):
                    c = b * HALVES + half
                    chunk(c, c + 1 if half + 1 < HALVES else (c + 1) % CHUNKS)
            sp.wait_ge(S_["y_loaded"], 16 * (CHUNKS + 1))
            sp.wait_ge(S_["out_stored"], 16 * CHUNKS)

        @block.gpsimd
        def _(pool):
            def chunk(c):
                S_.await_(pool, "acc_read", c, KT)
                pool.tensor_tensor(xn[:, :, :], xn[:, :, :], g[:, :, :], ALU.mult).then_inc(S_["gated"], 1)
                S_.await_(pool, "gated", c, 1)
                pool.tensor_tensor(xn[:, :, :], xn[:, :, :], x[:, :, :], ALU.add).then_inc(S_["out_ready"], 1)

            for half in range(HALVES):
                chunk(half)
            with pool.Fori(1, B) as b:
                for half in range(HALVES):
                    chunk(b * HALVES + half)

        @block.scalar
        def _(act):
            def split_swi(c, j):
                S_.await_(act, "g_mm", c, j - 1)
                act.activation(swi_hi[:, j % 2, :], swi[:, j % NJ, :], ACT.Copy).then_inc(S_["swi_hi"], 1)

            def split_out(c, j):
                S_.await_(act, "down_done", c, j - 1)
                act.activation(out_hi[:, j % 2, :], wout[:, j, :], ACT.Copy).then_inc(S_["out_hi"], 1)

            def high_y(c, slot):
                S_.await_(act, "y_loaded", c + 1, 16)
                S_.await_(act, "g_mm", c, 0)
                act.activation(yh[:, slot, :, :], y[:, :, :], ACT.Copy).then_inc(S_["yh_done"], 1)

            act.preload_act_table(ACT.Silu)
            high_y(-1, 0)
            act.wait_ge(swi_in[0], 16)
            split_swi(0, 0)

            def chunk(c, half, first):
                for j in range(NJ + 1):
                    if j < NJ:
                        if first and j + 1 < NJ:
                            act.wait_ge(swi_in[j + 1], 16)
                        split_swi(c, j + 1)
                        S_.await_(act, "u_mm", c, j + 1)
                        S_.await_(act, "h_done", c, j - 1)
                        act.activation(s_act[:, j % 2, :], ring[2 * j % 4][:, :], ACT.Silu)\
                            .then_inc(S_["s_done"], 1)
                    if j >= 1:
                        i = j - 1
                        S_.await_(act, "h_done", c, i + 1)
                        S_.await_(act, "down_done", c, i - 2)
                        act.activation(hh[:, i % 3, :], h[:, i % 2, :], ACT.Copy).then_inc(S_["hh_done"], 1)
                        if first:
                            act.wait_ge(out_in[i], 16)
                        split_out(c, i)
                    if j == 8:
                        high_y(c, 1 - half)

            for half in range(HALVES):
                chunk(half, half, half == 0)
            with act.Fori(1, B) as b:
                for half in range(HALVES):
                    chunk(b * HALVES + half, half, False)

        @block.vector
        def _(dve):
            def rest_swi(c, j):
                S_.await_(dve, "swi_hi", c, j + 1)
                S_.await_(dve, "g_mm", c, j - 1)
                dve.tensor_tensor(swi_lo[:, j % 2, :], swi[:, j % NJ, :], swi_hi[:, j % 2, :].bitcast(F32),
                                  ALU.subtract).then_inc(S_["swi_lo"], 1)

            def rest_out(c, j):
                S_.await_(dve, "out_hi", c, j + 1)
                S_.await_(dve, "down_done", c, j - 1)
                dve.tensor_tensor(out_lo[:, j % 2, :], wout[:, j, :], out_hi[:, j % 2, :].bitcast(F32),
                                  ALU.subtract).then_inc(S_["out_lo"], 1)

            def rest_y(c, slot):
                S_.await_(dve, "yh_done", c + 1, 1)
                dve.tensor_tensor(yl[:, slot, :, :], y[:, :, :], yh[:, slot, :, :].bitcast(F32),
                                  ALU.subtract).then_inc(S_["yl_done"], 1)

            rest_y(-1, 0)
            rest_swi(0, 0)

            def chunk(c, half):
                for j in range(NJ + 1):
                    if j < NJ:
                        rest_swi(c, j + 1)
                        S_.await_(dve, "s_done", c, j + 1)
                        S_.await_(dve, "g_mm", c, j + 1)
                        S_.await_(dve, "hh_done", c, j - 1)
                        S_.await_(dve, "hl_done", c, j - 1)
                        dve.tensor_tensor(h[:, j % 2, :], s_act[:, j % 2, :], ring[(2 * j + 1) % 4][:, :],
                                          ALU.mult).then_inc(S_["h_done"], 1)
                    if j >= 1:
                        i = j - 1
                        S_.await_(dve, "hh_done", c, i + 1)
                        S_.await_(dve, "down_done", c, i - 2)
                        dve.tensor_tensor(hl[:, i % 3, :], h[:, i % 2, :], hh[:, i % 3, :].bitcast(F32),
                                          ALU.subtract).then_inc(S_["hl_done"], 1)
                        rest_out(c, i)
                    if j == 8:
                        rest_y(c, 1 - half)
                S_.await_(dve, "down_done", c, NJ)
                S_.await_(dve, "tail_loaded", c, 48)
                for t in range(KT):
                    dve.tensor_tensor(xn[:, t, :], xn[:, t, :], acc[t][:, :], ALU.add)\
                        .then_inc(S_["acc_read"], 1)

            for half in range(HALVES):
                chunk(half, half)
            with dve.Fori(1, B) as b:
                for half in range(HALVES):
                    chunk(b * HALVES + half, half)

        @block.tensor
        def _(pe):
            def chunk(c, half):
                S_.await_(pe, "yh_done", c, 1)
                S_.await_(pe, "yl_done", c, 1)
                for j in range(NJ + LAG):
                    if j < NJ:
                        S_.await_(pe, "swi_hi", c, j + 1)
                        S_.await_(pe, "swi_lo", c, j + 1)
                        for which in range(2):
                            S_.await_(pe, ("s_done", "h_done")[which], c, j - 1)
                            i = 0
                            for k in range(KT):
                                col = ((1 - which) * KT + k) * P
                                for w, a in ((swi_hi, yh), (swi_hi, yl), (swi_lo, yh)):
                                    last = pe.matmul(ring[(2 * j + which) % 4][:, :], w[:, j % 2, col:col + P],
                                                     a[:, half, k, :], start=(i == 0), stop=(i == 3 * KT - 1))
                                    i += 1
                            last.then_inc(S_[("u_mm", "g_mm")[which]], 1)
                    if j >= LAG:
                        i = j - LAG
                        S_.await_(pe, "hl_done", c, i + 1)
                        S_.await_(pe, "out_lo", c, i + 1)
                        if i == 0:
                            S_.await_(pe, "acc_read", c, 0)
                        for t in range(KT):
                            n = 0
                            for w, a in ((out_hi, hh), (out_hi, hl), (out_lo, hh)):
                                last = pe.matmul(acc[t][:, :], w[:, i % 2, t * P:(t + 1) * P], a[:, i % 3, :],
                                                 start=(i == 0 and n == 0), stop=(i == NJ - 1 and n == 2))
                                n += 1
                        last.then_inc(S_["down_done"], 1)

            for half in range(HALVES):
                chunk(half, half)
            with pe.Fori(1, B) as b:
                for half in range(HALVES):
                    chunk(b * HALVES + half, half)


def build(nc, x_d, wqkv_d, wswi_d, wout_d, up_d, gate_d, down_d, out_d):
    shape = (CHUNKS, P, KT, T)
    xn_d, y_d, g_d = (nc.dram_tensor(n, shape, F32, kind="Internal").ap() for n in ("xn_dram", "y_dram", "g_dram"))
    phase_a(nc, x_d, wqkv_d, (up_d, gate_d, down_d), xn_d, y_d, g_d)
    phase_b(nc, x_d, wswi_d, wout_d, xn_d, y_d, g_d, out_d)


def kernel(**inputs):
    import numpy as np
    import concourse.bacc as bacc
    from concourse.bass_utils import run_bass_kernel_spmd as run

    def a(name):
        return np.ascontiguousarray(inputs[name])

    def lay(v):
        return np.ascontiguousarray(v)

    x = lay(a("L0_attn_x").reshape(CHUNKS, T, KT, P).transpose(0, 3, 2, 1))
    wqkv = lay(a("L0_attn_w_qkv").reshape(4, 3, P, KT, P).transpose(0, 4, 1, 3, 2)).reshape(4, P, 3 * KT * P)
    wswi = lay(a("L0_attn_w_swiglu").reshape(2, NJ, P, KT, P).transpose(1, 4, 0, 3, 2)).reshape(NJ, P, 2 * KT * P)
    wout = lay(a("L0_attn_w_out").reshape(D, NJ, P).transpose(1, 2, 0))
    up, gate = (lay(a(n).reshape(NJ // 2, 2, P, KT, P).transpose(0, 4, 1, 3, 2)).reshape(NJ // 2, P, 2 * KT * P)
                for n in ("L0_ffn_W_up", "L0_ffn_W_gate"))
    down = lay(a("L0_ffn_W_down").reshape(D, NJ // 2, 2, P).transpose(1, 3, 2, 0)).reshape(NJ // 2, P, 2 * D)

    nc = bacc.Bacc("TRN2", target_bir_lowering=False, num_devices=1)
    arrays = {"x": x, "wqkv": wqkv, "wswi": wswi, "wout": wout, "up": up, "gate": gate, "down": down}
    args = [nc.dram_tensor("in_" + n, v.shape, F32, kind="ExternalInput").ap() for n, v in arrays.items()]
    out = nc.dram_tensor("out_x", (CHUNKS, P, KT, T), F32, kind="ExternalOutput").ap()
    build(nc, *args, out)
    r = run(nc, [{"in_" + n: v for n, v in arrays.items()}], core_ids=[0])
    got = r.results[0]["out_x"]
    return lay(got.transpose(0, 3, 2, 1)).reshape(B, S, D)
```

```python
from contextlib import ExitStack

import concourse.bass as bass
from concourse import mybir

F32 = mybir.dt.float32
F32R = mybir.dt.float32r
F16 = mybir.dt.float16
U32 = mybir.dt.uint32
ALU = mybir.AluOpType
ACT = mybir.ActivationFunctionType
AX = mybir.AxisListType
RMAX = bass.bass_isa.ReduceOp.max

P = 128
B, S, D = 4, 1024, 512
E = 2048
T = 512
HALVES = S // T
CHUNKS = B * HALVES
KT = D // P
NJ = E // P
M3 = 3 * KT
LN_EPS = 1e-5
RMS_EPS = 1.1920929e-07
QUANT_EPS = 1e-8
DEN_EPS = 1e-6
LAG = 2
GRAN = 256

XS = 2.0 ** 10
HS = 2.0 ** -14
TERN = (1.0, 2.0, 2.0)
WTOP = 2.0 ** 14

QKV_ORDER = list(range(KT, 2 * KT)) + list(range(0, KT)) + list(range(2 * KT, 3 * KT))
K0, Q0, V0 = 0, KT, 2 * KT


class Signals:

    def __init__(self, nc, ctx, per_chunk, prefix=""):
        self.per = per_chunk
        self.sem = {n: ctx.enter_context(nc.semaphore(prefix + n)) for n in per_chunk}

    def __getitem__(self, name):
        return self.sem[name]

    def at(self, name, c, k):
        return c * self.per[name] + k

    def await_(self, eng, name, c, k):
        v = self.at(name, c, k)
        if isinstance(v, int) and v <= 0:
            return
        eng.wait_ge(self.sem[name], v)


def phase_a(nc, x_d, wqkv_d, ternary_d, xn_d, y_d, g_d):
    with ExitStack() as ctx:
        def sb(name, shape, dt):
            return ctx.enter_context(nc.sbuf_tensor("a_" + name, shape, dt))

        def pb(name):
            return ctx.enter_context(nc.psum_tensor("a_" + name, [P, T], F32))

        def sem(name):
            return ctx.enter_context(nc.semaphore("a_" + name))

        wq_hi = sb("wq_hi", [P, M3, KT, P], F16)
        wq_lo = sb("wq_lo", [P, M3, KT, P], F16)
        tern = [sb(n, [P, NJ * KT * P], F16) for n in ("tern_up", "tern_gate", "tern_down")]
        x = sb("x", [P, KT, T], F32)
        xh = sb("xh", [P, 2, KT, T], F16)
        xl = sb("xl", [P, 2, KT, T], F16)
        kqv = sb("kqv", [P, M3, T], F32)
        sq = sb("sq", [P, KT, T], F32)
        add2 = sb("add2", [P, 2, T], F32)
        add1 = sb("add1", [P, T], F32)
        var2 = sb("var2", [P, 2, T], F32)
        inv2 = sb("inv2", [P, 2, T], F32)
        r_t = sb("r_t", [P, T], F32)
        m2 = sb("m2", [P, T], F32)
        kq_ms = sb("kq_ms", [P, 2, T], F32)
        s_act = sb("s_act", [P, 2, T], F32)
        h = sb("h", [P, 2, T], F32)
        hh = sb("hh", [P, 3, T], F16)
        hl = sb("hl", [P, 3, T], F16)
        g_out = sb("g_out", [P, KT, T], F32)
        RING = 4
        sign_hi = sb("sign_hi", [P, 2, 1024], F16)
        sign_lo = sb("sign_lo", [P, 2, 1024], F16)
        stage = sb("stage", [P, RING, 1024], F32)
        below = sb("below", [P, 2, 1024], F16)
        mean_w = sb("mean_w", [P, P], F32)
        count_w = sb("count_w", [P, P], F32)
        one_col = sb("one_col", [P, 1], F32)
        carry = sb("carry", [P, 2, KT], F32)
        absum = sb("absum", [P, 3, 8], F32)
        absum3 = sb("absum3", [P, 3], F32)
        absjunk = sb("absjunk", [P, 1024], F16)
        scale3 = sb("scale3", [P, 3], F32)
        half3 = sb("half3", [P, 3], F32)
        nhalf3 = sb("nhalf3", [P, 3], F32)
        c_up = sb("c_up", [P, 1], F32)
        inv_up = sb("inv_up", [P, 2], F32)
        c_ffn = sb("c_ffn", [P, 3], F32)
        wmax = sb("wmax", [P, 6], F32)
        wpow = sb("wpow", [P, 1], F32)
        s_w = sb("s_w", [P, 2], F32)
        c_w = sb("c_w", [P, 1], F32)

        ring = [pb(f"ring{i}") for i in range(3)]
        acc = [pb(f"acc{i}") for i in range(KT)]
        stat = pb("stat")

        S_ = Signals(nc, ctx, {
            "x_loaded": 16, "xn_stored": 16, "y_stored": 16, "g_stored": 16,
            "fold_half": 4, "fold_done": 4, "stat_mm": 4, "stat_read": 4, "sq_done": 3,
            "centred": 1, "var_root": 1, "inv_x": 2 * T // GRAN, "norms": 3, "xh_done": 1, "xl_done": 1,
            "qkv_mm": M3, "qkv_read": M3, "kq_root": 1, "inv_kq": 2 * T // GRAN, "kq_scaled": 2 * KT,
            "exped": 2, "wv_done": KT, "summed": 2 * KT + 2, "den_done": 1, "inv_den": KT * T // GRAN,
            "y_done": KT, "u_mm": NJ, "g_mm": NJ, "s_done": NJ, "h_done": NJ, "hh_done": NJ, "hl_done": NJ,
            "down_done": NJ, "g_act": KT,
        }, "a_")
        wq_in = [sem(f"wq_in{i}") for i in range(4)]
        stage_in = [sem(f"stage_in{i}") for i in range(RING)]
        stage_free = [sem(f"stage_free{i}") for i in range(RING)]
        signs_s = sem("signs")
        consts = sem("consts")
        wmax_s = sem("wmax")
        wscale = sem("wscale")
        wq_hi_s = sem("wq_hi")
        wq_lo_s = sem("wq_lo")
        absum_s = sem("absum")
        absdone = sem("absdone")
        mean3_s = sem("mean3")
        scales_s = sem("scales")
        below_s = sem("below")
        tern_s = sem("tern")

        wq_raw = kqv
        wq_raw_f = wq_raw[:, :, :].rearrange("p a b -> p (a b)")
        wq_hi_f = wq_hi[:, :, :, :].rearrange("p a b c -> p (a b c)")
        wq_lo_f = wq_lo[:, :, :, :].rearrange("p a b c -> p (a b c)")
        WQ = M3 * D // 4
        up = tern[0][:, :].rearrange("p (j k m) -> p j k m", j=NJ, k=KT)
        gate = tern[1][:, :].rearrange("p (j k m) -> p j k m", j=NJ, k=KT)
        down = tern[2][:, :].rearrange("p (j n) -> p j n", j=NJ)
        pieces = [(m, g) for m in range(3) for g in range(8)] + [(m, g) for g in range(8) for m in range(3)]
        NSUM = 24
        WQ_ORDER = (1, 2, 0, 3)
        QUANT_AT = {-1: (0, 1), 1: (2,), 3: (3,), 5: (4,), 7: (5,), 9: (6,), 11: (7,)}

        def piece_in(eng, n):
            eng.wait_ge(stage_in[n % RING], 16 * (n // RING + 1))

        def wide(t):
            return t.unsqueeze(1).to_broadcast([P, KT, T])

        block = ctx.enter_context(nc.Block())

        @block.sync
        def _(sp):
            sp.dma_start(x[:, :, :], x_d[0]).then_inc(S_["x_loaded"], 16)
            for i in WQ_ORDER:
                sp.dma_start(wq_raw_f[:, i * WQ:(i + 1) * WQ], wqkv_d[i]).then_inc(wq_in[i], 16)

            def load_pieces(first, last):
                for n in range(first, last):
                    m, g = pieces[n]
                    if n >= RING:
                        sp.wait_ge(stage_free[n % RING], n // RING)
                    sp.dma_start(stage[:, n % RING, :], ternary_d[m][g]).then_inc(stage_in[n % RING], 16)

            def next_x(c, nxt):
                S_.await_(sp, "norms", c, 3)
                sp.dma_start(xn_d[bass.ds(c, 1)].rearrange("c p k t -> p (c k) t"), x[:, :, :])\
                    .then_inc(S_["xn_stored"], 16)
                S_.await_(sp, "xh_done", c, 1)
                S_.await_(sp, "xl_done", c, 1)
                S_.await_(sp, "xn_stored", c, 16)
                sp.dma_start(x[:, :, :], x_d[bass.ds(nxt, 1)].rearrange("c p k t -> p (c k) t"))\
                    .then_inc(S_["x_loaded"], 16)

            def results(c):
                S_.await_(sp, "y_done", c, KT)
                sp.dma_start(y_d[bass.ds(c, 1)].rearrange("c p k t -> p (c k) t"), kqv[:, V0:V0 + KT, :])\
                    .then_inc(S_["y_stored"], 16)
                S_.await_(sp, "g_act", c, KT)
                sp.dma_start(g_d[bass.ds(c, 1)].rearrange("c p k t -> p (c k) t"), g_out[:, :, :])\
                    .then_inc(S_["g_stored"], 16)

            load_pieces(0, NSUM)
            next_x(0, 1)
            load_pieces(NSUM, len(pieces))
            results(0)
            for c in range(1, HALVES):
                next_x(c, c + 1)
                results(c)
            with sp.Fori(1, B) as b:
                for half in range(HALVES):
                    c = b * HALVES + half
                    next_x(c, c + 1 if half + 1 < HALVES else (c + 1) % CHUNKS)
                    results(c)
            sp.wait_ge(S_["x_loaded"], 16 * (CHUNKS + 1))
            for name in ("xn_stored", "y_stored", "g_stored"):
                sp.wait_ge(S_[name], 16 * CHUNKS)

        @block.gpsimd
        def _(pool):
            pool.memset(mean_w[:, :], 1.0 / D).then_inc(consts, 1)
            pool.memset(count_w[:, :], 1.0 / (E * D)).then_inc(consts, 1)
            pool.memset(one_col[:, :], 1.0).then_inc(consts, 1)

            def fold(c, k, src):
                S_.await_(pool, "stat_mm", c, k - 1)
                S_.await_(pool, "fold_done", c, k - 1)
                pool.tensor_tensor(add2[:, :, :], src[:, 0:2, :], src[:, 2:4, :], ALU.add)\
                    .then_inc(S_["fold_half"], 1)
                S_.await_(pool, "fold_half", c, k)
                pool.tensor_tensor(add1[:, :], add2[:, 0, :], add2[:, 1, :], ALU.add)\
                    .then_inc(S_["fold_done"], 1)

            S_.await_(pool, "x_loaded", 0, 16)
            fold(0, 1, x)
            pool.wait_ge(wmax_s, 5)
            pool.partition_all_reduce(wmax[:, 5:6], wmax[:, 4:5], P, RMAX).then_inc(wmax_s, 1)
            S_.await_(pool, "sq_done", 0, 1)
            fold(0, 2, sq)

            def quantise(g):
                n = NSUM + 3 * g
                piece_in(pool, n)
                if g >= 2:
                    pool.wait_ge(tern_s, 3 * (g - 2) + 1)
                pool.tensor_scalar(below[:, g % 2, :], stage[:, n % RING, :], nhalf3[:, 0:1], None, ALU.is_lt)\
                    .then_inc(below_s, 1)

            def chunk(c, first=False):
                S_.await_(pool, "sq_done", c, 2)
                fold(c, 3, sq)
                S_.await_(pool, "sq_done", c, 3)
                fold(c, 4, sq)
                S_.await_(pool, "x_loaded", c + 1, 16)
                fold(c, 5, x)
                if first:
                    pool.wait_ge(scales_s, 6)
                    for g in QUANT_AT[-1]:
                        quantise(g)

                def scale_kq(t):
                    which = t // KT
                    S_.await_(pool, "inv_kq", c, (which + 1) * (T // GRAN))
                    pool.tensor_tensor(kqv[:, t, :], kqv[:, t, :], kq_ms[:, which, :], ALU.mult)\
                        .then_inc(S_["kq_scaled"], 1)

                def wv(t):
                    S_.await_(pool, "exped", c, 1)
                    pool.tensor_tensor(kqv[:, V0 + t, :], kqv[:, V0 + t, :], kqv[:, K0 + t, :], ALU.mult)\
                        .then_inc(S_["wv_done"], 1)

                def y(t):
                    S_.await_(pool, "inv_den", c, (t + 1) * (T // GRAN))
                    pool.tensor_tensor(kqv[:, V0 + t, :], kqv[:, V0 + t, :], kqv[:, Q0 + t, :], ALU.mult)\
                        .then_inc(S_["y_done"], 1)

                def var_fold():
                    S_.await_(pool, "sq_done", c, 4)
                    fold(c, 6, sq)

                jobs = {1: [(scale_kq, 0), (scale_kq, 1)], 2: [(scale_kq, 2), (scale_kq, 3)],
                        3: [(scale_kq, 4), (scale_kq, 5)], 4: [(scale_kq, 6), (scale_kq, 7)],
                        5: [(wv, 0), (wv, 1)], 6: [(wv, 2), (wv, 3)], 7: [(var_fold,)],
                        16: [(y, 0), (y, 1), (y, 2), (y, 3)]}
                for j in range(NJ + 1):
                    if j >= 1:
                        i = j - 1
                        S_.await_(pool, "hh_done", c, i + 1)
                        S_.await_(pool, "down_done", c, i - 2)
                        pool.tensor_tensor(hl[:, i % 3, :], h[:, i % 2, :], hh[:, i % 3, :], ALU.subtract)\
                            .then_inc(S_["hl_done"], 1)
                    for job in jobs.get(j, []):
                        job[0](*job[1:])
                    if first:
                        for g in QUANT_AT.get(j, ()):
                            quantise(g)

            for half in range(HALVES):
                chunk(half, half == 0)
            with pool.Fori(1, B) as b:
                for half in range(HALVES):
                    chunk(b * HALVES + half)

        @block.scalar
        def _(act):
            def roots(c):
                S_.await_(act, "stat_read", c, 6)
                act.activation(var2[:, :, :], var2[:, :, :], ACT.Sqrt).then_inc(S_["var_root"], 1)

            def square_x(c, k):
                S_.await_(act, "centred", c + 1, 1)
                S_.await_(act, "fold_half", c, k)
                act.activation(sq[:, :, :], x[:, :, :], ACT.Square).then_inc(S_["sq_done"], 1)

            def high_x(c, slot):
                S_.await_(act, "norms", c + 1, 3)
                S_.await_(act, "g_mm", c, 0)
                act.activation(xh[:, slot, :, :], x[:, :, :], ACT.Copy, scale=XS).then_inc(S_["xh_done"], 1)

            S_.await_(act, "centred", 0, 1)
            act.activation(sq[:, :, :], x[:, :, :], ACT.Square).then_inc(S_["sq_done"], 1)
            act.wait_ge(wscale, 3)
            for i in WQ_ORDER:
                act.activation(wq_hi_f[:, i * WQ:(i + 1) * WQ], wq_raw_f[:, i * WQ:(i + 1) * WQ], ACT.Copy,
                               scale=s_w[:, 0:1]).then_inc(wq_hi_s, 1)
            roots(-1)
            high_x(-1, 0)

            def abs_sum(n):
                m, g = pieces[n]
                piece_in(act, n)
                if n >= 1:
                    act.wait_ge(absdone, n)
                act.activation(absjunk[:, :], stage[:, n % RING, :], ACT.Abs,
                               accum_out=absum[:, m, g:g + 1]).then_inc(absdone, 1)
                act.wait_ge(absdone, n + 1)
                act.sem_inc(stage_free[n % RING], 1)

            def quantise(g):
                for m in (1, 2):
                    n, i = NSUM + 3 * g + m, 2 * g + m - 1
                    piece_in(act, n)
                    if i >= 2:
                        act.wait_ge(tern_s, 3 * ((i - 2) // 2) + 2 + (i - 2) % 2)
                    act.activation(sign_hi[:, i % 2, :], stage[:, n % RING, :], ACT.Sign, bias=nhalf3[:, m:m + 1],
                                   scale=1.0 - 2.0 ** -24)
                    act.activation(sign_lo[:, i % 2, :], stage[:, n % RING, :], ACT.Sign, bias=half3[:, m:m + 1],
                                   scale=1.0 - 2.0 ** -24).then_inc(signs_s, 1)
                    act.wait_ge(signs_s, i + 1)
                    act.sem_inc(stage_free[n % RING], 1)

            def chunk(c, half, first=False):
                if first:
                    for n in range(12):
                        abs_sum(n)
                S_.await_(act, "qkv_read", c, KT)
                S_.await_(act, "fold_half", c, 2)
                act.activation(sq[:, :, :], kqv[:, K0:K0 + KT, :], ACT.Square).then_inc(S_["sq_done"], 1)
                if first:
                    for n in range(12, NSUM):
                        abs_sum(n)
                S_.await_(act, "qkv_read", c, 2 * KT)
                S_.await_(act, "fold_half", c, 3)
                act.activation(sq[:, :, :], kqv[:, Q0:Q0 + KT, :], ACT.Square).then_inc(S_["sq_done"], 1)
                if first:
                    act.wait_ge(scales_s, 6)
                    for g in QUANT_AT[-1]:
                        quantise(g)
                S_.await_(act, "stat_read", c, 4)
                act.activation(kq_ms[:, :, :], kq_ms[:, :, :], ACT.Sqrt).then_inc(S_["kq_root"], 1)

                def exp_kq():
                    S_.await_(act, "kq_scaled", c, KT)
                    act.activation(kqv[:, K0:K0 + KT, :], kqv[:, K0:K0 + KT, :], ACT.Exp)\
                        .then_inc(S_["exped"], 1)
                    S_.await_(act, "kq_scaled", c, 2 * KT)
                    act.activation(kqv[:, Q0:Q0 + KT, :], kqv[:, Q0:Q0 + KT, :], ACT.Exp, scale=-1.0)\
                        .then_inc(S_["exped"], 1)

                jobs = {3: (square_x, c, 4), 5: (exp_kq,), 9: (roots, c), 14: (high_x, c, 1 - half)}
                for j in range(NJ + 1):
                    if j < NJ:
                        S_.await_(act, "u_mm", c, j + 1)
                        S_.await_(act, "h_done", c, j - 1)
                        act.activation(s_act[:, j % 2, :], ring[2 * j % 3][:, :], ACT.Silu, scale=c_up[:, 0:1])\
                            .then_inc(S_["s_done"], 1)
                    if j >= 1:
                        i = j - 1
                        S_.await_(act, "h_done", c, i + 1)
                        S_.await_(act, "down_done", c, i - 2)
                        act.activation(hh[:, i % 3, :], h[:, i % 2, :], ACT.Copy).then_inc(S_["hh_done"], 1)
                    if j in jobs:
                        jobs[j][0](*jobs[j][1:])
                    if first:
                        for g in QUANT_AT.get(j, ()):
                            quantise(g)
                S_.await_(act, "down_done", c, NJ)
                S_.await_(act, "g_stored", c, 0)
                for t in range(KT):
                    act.activation(g_out[:, t, :], acc[t][:, :], ACT.Silu, scale=c_ffn[:, 2:3])\
                        .then_inc(S_["g_act"], 1)

            for half in range(HALVES):
                chunk(half, half, half == 0)
            with act.Fori(1, B) as b:
                for half in range(HALVES):
                    chunk(b * HALVES + half, half)

        @block.vector
        def _(dve):
            PER_T = T // GRAN

            def centre(c):
                S_.await_(dve, "stat_mm", c, 5)
                S_.await_(dve, "x_loaded", c + 1, 16)
                dve.tensor_tensor(x[:, :, :], x[:, :, :], wide(stat[:, :]), ALU.subtract)\
                    .then_inc(S_["centred"], 1)
                S_.await_(dve, "centred", c + 1, 1)
                dve.sem_inc(S_["stat_read"], 1)

            def variances(c):
                S_.await_(dve, "stat_mm", c, 6)
                S_.await_(dve, "norms", c + 1, 0)
                dve.tensor_scalar(var2[:, 0, :], stat[:, :], LN_EPS, None, ALU.add)
                dve.tensor_scalar(var2[:, 1, :], stat[:, :], 1.0 + RMS_EPS, RMS_EPS * LN_EPS,
                                  ALU.mult, ALU.add).then_inc(S_["stat_read"], 1)

            def invert_x(c, g):
                i, o = g // PER_T, g % PER_T * GRAN
                S_.await_(dve, "var_root", c + 1, 1)
                dve.reciprocal(inv2[:, i, o:o + GRAN], var2[:, i, o:o + GRAN]).then_inc(S_["inv_x"], 1)

            def norms(c):
                S_.await_(dve, "inv_x", c + 1, 2 * PER_T)
                dve.tensor_tensor(r_t[:, :], var2[:, 0, :], inv2[:, 1, :], ALU.mult)
                dve.tensor_tensor(m2[:, :], var2[:, 1, :], inv2[:, 0, :], ALU.mult).then_inc(S_["norms"], 1)
                S_.await_(dve, "norms", c + 1, 1)
                dve.tensor_tensor(m2[:, :], m2[:, :], m2[:, :], ALU.mult).then_inc(S_["norms"], 1)
                dve.tensor_tensor(x[:, :, :], x[:, :, :], wide(inv2[:, 0, :]), ALU.mult)\
                    .then_inc(S_["norms"], 1)

            def low_x(c, slot):
                S_.await_(dve, "norms", c + 1, 3)
                S_.await_(dve, "xh_done", c + 1, 1)
                dve.scalar_tensor_tensor(xl[:, slot, :, :], x[:, :, :], XS, xh[:, slot, :, :],
                                         ALU.mult, ALU.subtract).then_inc(S_["xl_done"], 1)

            centre(-1)
            for n, i in enumerate(WQ_ORDER):
                dve.wait_ge(wq_in[i], 16)
                dve.tensor_reduce(wmax[:, i:i + 1], wq_raw_f[:, i * WQ:(i + 1) * WQ], AX.X, ALU.max,
                                  apply_absolute_value=True).then_inc(wmax_s, 1)
            dve.wait_ge(wmax_s, 4)
            dve.tensor_reduce(wmax[:, 4:5], wmax[:, 0:4], AX.X, ALU.max).then_inc(wmax_s, 1)
            dve.wait_ge(wmax_s, 6)
            dve.tensor_scalar(wpow[:, :], wmax[:, 5:6], 1e-30, None, ALU.max).then_inc(wscale, 1)
            dve.wait_ge(wscale, 1)
            dve.tensor_scalar(c_w[:, :].bitcast(U32), wpow[:, :].bitcast(U32), 0x7F800000, None,
                              ALU.bitwise_and).then_inc(wscale, 1)
            dve.wait_ge(wscale, 2)
            dve.reciprocal(s_w[:, 1:2], c_w[:, :]).then_inc(wq_lo_s, 1)
            dve.wait_ge(wq_lo_s, 1)
            dve.tensor_scalar(s_w[:, 0:1], s_w[:, 1:2], WTOP, None, ALU.mult).then_inc(wscale, 1)
            dve.tensor_scalar(c_w[:, :], c_w[:, :], 1.0 / (WTOP * XS), None, ALU.mult).then_inc(wscale, 1)
            dve.wait_ge(wscale, 4)
            variances(-1)
            for g in range(2 * PER_T):
                invert_x(-1, g)
            norms(-1)
            low_x(-1, 0)
            for n, i in enumerate(WQ_ORDER):
                dve.wait_ge(wq_hi_s, n + 1)
                dve.scalar_tensor_tensor(wq_lo_f[:, i * WQ:(i + 1) * WQ], wq_raw_f[:, i * WQ:(i + 1) * WQ],
                                         s_w[:, 0:1], wq_hi_f[:, i * WQ:(i + 1) * WQ],
                                         ALU.mult, ALU.subtract).then_inc(wq_lo_s, 1)

            def scales():
                dve.wait_ge(mean3_s, 1)
                dve.tensor_scalar(scale3[:, :], stat[:, 0:3], QUANT_EPS, None, ALU.add).then_inc(absum_s, 1)
                dve.wait_ge(absum_s, 2)
                dve.tensor_scalar(half3[:, :], scale3[:, :], 0.5, None, ALU.mult).then_inc(scales_s, 1)
                dve.tensor_scalar(nhalf3[:, :], scale3[:, :], -0.5, None, ALU.mult).then_inc(scales_s, 1)
                dve.tensor_scalar(c_up[:, :], scale3[:, 0:1], 1.0 / (XS * TERN[0]), None, ALU.mult)\
                    .then_inc(scales_s, 1)
                dve.reciprocal(inv_up[:, 0:1], scale3[:, 0:1]).then_inc(absum_s, 1)
                dve.tensor_tensor(c_ffn[:, 0:1], scale3[:, 0:1], scale3[:, 1:2], ALU.mult).then_inc(absum_s, 1)
                dve.wait_ge(absum_s, 4)
                dve.tensor_scalar(inv_up[:, 1:2], inv_up[:, 0:1], HS, None, ALU.mult).then_inc(scales_s, 1)
                dve.tensor_tensor(c_ffn[:, 1:2], c_ffn[:, 0:1], scale3[:, 2:3], ALU.mult).then_inc(scales_s, 1)
                dve.wait_ge(scales_s, 5)
                dve.tensor_scalar(c_ffn[:, 2:3], c_ffn[:, 1:2], 1.0 / (HS * XS * TERN[1] * TERN[2]), None, ALU.mult)\
                    .then_inc(scales_s, 1)
                dve.wait_ge(scales_s, 6)

            def quantise(g):
                n, cols = NSUM + 3 * g, slice(g * 1024, (g + 1) * 1024)
                dve.wait_ge(below_s, g + 1)
                dve.scalar_tensor_tensor(tern[0][:, cols], stage[:, n % RING, :], half3[:, 0:1],
                                         below[:, g % 2, :], ALU.is_gt, ALU.subtract).then_inc(tern_s, 1)
                dve.wait_ge(tern_s, 3 * g + 1)
                dve.sem_inc(stage_free[n % RING], 1)
                for m in (1, 2):
                    i = 2 * g + m - 1
                    dve.wait_ge(signs_s, i + 1)
                    dve.tensor_tensor(tern[m][:, cols], sign_hi[:, i % 2, :], sign_lo[:, i % 2, :], ALU.add)\
                        .then_inc(tern_s, 1)

            def chunk(c, half, first=False):
                def read_qkv(n):
                    S_.await_(dve, "qkv_mm", c, n + 1)
                    if n < 2 * KT:
                        if n >= KT:
                            S_.await_(dve, "y_done", c, 0)
                        dve.tensor_scalar(kqv[:, n, :], ring[n % 3][:, :], c_w[:, 0:1], None, ALU.mult)\
                            .then_inc(S_["qkv_read"], 1)
                    else:
                        S_.await_(dve, "y_stored", c, 0)
                        dve.scalar_tensor_tensor(kqv[:, n, :], ring[n % 3][:, :], c_w[:, 0:1], r_t[:, :],
                                                 ALU.mult, ALU.mult).then_inc(S_["qkv_read"], 1)

                def mean_square(which):
                    S_.await_(dve, "stat_mm", c, 3 + which)
                    dve.scalar_tensor_tensor(kq_ms[:, which, :], m2[:, :], RMS_EPS, stat[:, :],
                                             ALU.mult, ALU.add).then_inc(S_["stat_read"], 1)

                S_.await_(dve, "den_done", c, 0)
                if first:
                    dve.wait_ge(wq_lo_s, 5)
                for n in range(M3):
                    read_qkv(n)
                    if n == 2 * KT:
                        mean_square(0)
                        if first:
                            dve.wait_ge(absdone, NSUM)
                            dve.tensor_reduce(absum3[:, :], absum[:, :, :], AX.X, ALU.add).then_inc(absum_s, 1)
                            scales()
                mean_square(1)
                if first:
                    for g in QUANT_AT[-1]:
                        quantise(g)

                def invert_kq(g):
                    i, o = g // PER_T, g % PER_T * GRAN
                    S_.await_(dve, "kq_root", c, 1)
                    dve.reciprocal(kq_ms[:, i, o:o + GRAN], kq_ms[:, i, o:o + GRAN]).then_inc(S_["inv_kq"], 1)

                def running_sum(n):
                    which, t = n // KT, n % KT
                    tile = (K0 if which == 0 else V0) + t
                    if which == 0:
                        S_.await_(dve, "wv_done", c, KT)
                    start = carry[:, which, t:t + 1] if half else (DEN_EPS if which == 0 else 0.0)
                    dve.tensor_tensor_scan(kqv[:, tile, :], one_col[:, 0:1].to_broadcast([P, T]),
                                           kqv[:, tile, :], start, ALU.mult, ALU.add)\
                        .then_inc(S_["summed"], 1)

                def keep_ends():
                    S_.await_(dve, "summed", c, 2 * KT)
                    for which, tile in ((0, K0), (1, V0)):
                        dve.tensor_copy(carry[:, which, :], kqv[:, tile:tile + KT, T - 1:T]
                                        .rearrange("p k o -> p (k o)")).then_inc(S_["summed"], 1)

                def denominators():
                    S_.await_(dve, "exped", c, 2)
                    S_.await_(dve, "summed", c, KT)
                    dve.scalar_tensor_tensor(kqv[:, Q0:Q0 + KT, :], kqv[:, Q0:Q0 + KT, :], 1.0,
                                             kqv[:, K0:K0 + KT, :], ALU.add, ALU.mult)\
                        .then_inc(S_["den_done"], 1)

                def invert_den(g):
                    t, o = Q0 + g // PER_T, g % PER_T * GRAN
                    S_.await_(dve, "den_done", c, 1)
                    S_.await_(dve, "summed", c, 2 * KT + 2)
                    dve.reciprocal(kqv[:, t, o:o + GRAN], kqv[:, t, o:o + GRAN]).then_inc(S_["inv_den"], 1)

                jobs = {0: [(invert_kq, 0), (invert_kq, 1)], 1: [(invert_kq, 2), (invert_kq, 3)],
                        2: [(centre, c)],
                        7: [(running_sum, 0), (running_sum, 1), (running_sum, 2)],
                        8: [(running_sum, 3), (running_sum, 4), (running_sum, 5)],
                        9: [(variances, c), (running_sum, 6), (running_sum, 7), (keep_ends,)],
                        10: [(denominators,), (invert_den, 0)],
                        11: [(invert_x, c, 0), (invert_x, c, 1)],
                        12: [(invert_x, c, 2), (invert_x, c, 3)],
                        13: [(norms, c)],
                        14: [(invert_den, 1), (invert_den, 2)],
                        15: [(low_x, c, 1 - half), (invert_den, 3)],
                        16: [(invert_den, 4), (invert_den, 5), (invert_den, 6), (invert_den, 7)]}
                for j in range(NJ + 1):
                    if j < NJ:
                        S_.await_(dve, "s_done", c, j + 1)
                        S_.await_(dve, "g_mm", c, j + 1)
                        S_.await_(dve, "hl_done", c, j - 1)
                        S_.await_(dve, "hh_done", c, j - 1)
                        dve.scalar_tensor_tensor(h[:, j % 2, :], s_act[:, j % 2, :], inv_up[:, 1:2],
                                                 ring[(2 * j + 1) % 3][:, :], ALU.mult, ALU.mult)\
                            .then_inc(S_["h_done"], 1)
                    for job in jobs.get(j, []):
                        job[0](*job[1:])
                    if first:
                        for g in QUANT_AT.get(j, ()):
                            quantise(g)

            for half in range(HALVES):
                chunk(half, half, half == 0)
            with dve.Fori(1, B) as b:
                for half in range(HALVES):
                    chunk(b * HALVES + half, half)

        @block.tensor
        def _(pe):
            def mean_over_features(c, k):
                S_.await_(pe, "fold_done", c, k)
                S_.await_(pe, "stat_read", c, k - 1)
                pe.matmul(stat[:, :], mean_w[:, :], add1[:, :], start=True, stop=True)\
                    .then_inc(S_["stat_mm"], 1)

            pe.wait_ge(consts, 3)
            mean_over_features(0, 1)
            mean_over_features(0, 2)

            def mean_of_weights():
                pe.wait_ge(absum_s, 1)
                S_.await_(pe, "stat_read", 0, 3)
                pe.matmul(stat[:, 0:3], count_w[:, :], absum3[:, :], start=True, stop=True).then_inc(mean3_s, 1)

            def chunk(c, half, first=False):
                S_.await_(pe, "xh_done", c, 1)
                S_.await_(pe, "xl_done", c, 1)
                for n, m in enumerate(QKV_ORDER):
                    if n >= 3:
                        S_.await_(pe, "qkv_read", c, n - 2)
                    elif n == 0:
                        S_.await_(pe, "s_done", c, 0)
                        S_.await_(pe, "h_done", c, 0)
                    if first:
                        pe.wait_ge(wq_lo_s, 2 + WQ_ORDER.index(m // 3))
                    i = 0
                    for k in range(KT):
                        for w, a in ((wq_hi, xh), (wq_hi, xl), (wq_lo, xh)):
                            last = pe.matmul(ring[n % 3][:, :], w[:, m, k, :], a[:, half, k, :],
                                             start=(i == 0), stop=(i == 3 * KT - 1))
                            i += 1
                    last.then_inc(S_["qkv_mm"], 1)
                    if n == 2 * KT:
                        mean_over_features(c, 3)
                    if first and n == 2 * KT + 1:
                        mean_of_weights()
                if first:
                    pe.wait_ge(absum_s, 2)
                mean_over_features(c, 4)

                def project(w, j, bank, done):
                    for i in range(2 * KT):
                        last = pe.matmul(bank[:, :], w[:, j, i // 2, :], (xh, xl)[i % 2][:, half, i // 2, :],
                                         start=(i == 0), stop=(i == 2 * KT - 1))
                    last.then_inc(S_[done], 1)

                for j in range(NJ + LAG):
                    if first and j < NJ and j % 2 == 0:
                        pe.wait_ge(tern_s, 3 * (j // 2) + 3)
                    if j < NJ:
                        for which in range(2):
                            m = 2 * j + which
                            if m < 3:
                                S_.await_(pe, "qkv_read", c, M3 - 2 + m)
                            elif (m - 3) % 2 == 0:
                                S_.await_(pe, "s_done", c, (m - 3) // 2 + 1)
                            else:
                                S_.await_(pe, "h_done", c, (m - 3) // 2 + 1)
                            project((up, gate)[which], j, ring[m % 3], ("u_mm", "g_mm")[which])
                    if j >= LAG:
                        i = j - LAG
                        S_.await_(pe, "hl_done", c, i + 1)
                        if i == 0:
                            S_.await_(pe, "g_act", c, 0)
                        for t in range(KT):
                            pe.matmul(acc[t][:, :], down[:, i, t * P:(t + 1) * P], hh[:, i % 3, :],
                                      start=(i == 0), stop=False)
                            last = pe.matmul(acc[t][:, :], down[:, i, t * P:(t + 1) * P], hl[:, i % 3, :],
                                             start=False, stop=(i == NJ - 1))
                        last.then_inc(S_["down_done"], 1)
                    if j == 1:
                        mean_over_features(c, 5)
                    if j == 8:
                        mean_over_features(c, 6)

            for half in range(HALVES):
                chunk(half, half, half == 0)
            with pe.Fori(1, B) as b:
                for half in range(HALVES):
                    chunk(b * HALVES + half, half)


def phase_b(nc, x_d, wswi_d, wout_d, xn_d, y_d, g_d, out_d):
    with ExitStack() as ctx:
        def sb(name, shape, dt):
            return ctx.enter_context(nc.sbuf_tensor("b_" + name, shape, dt))

        def pb(name):
            return ctx.enter_context(nc.psum_tensor("b_" + name, [P, T], F32))

        def sem(name):
            return ctx.enter_context(nc.semaphore("b_" + name))

        UNIT = 2 * KT * P
        swi = sb("swi", [P, NJ, UNIT], F32)
        wout = sb("wout", [P, NJ, D], F32)
        swi_hi = sb("swi_hi", [P, 2, UNIT], F32R)
        swi_lo = sb("swi_lo", [P, 2, UNIT], F32R)
        out_hi = sb("out_hi", [P, 2, D], F32R)
        out_lo = sb("out_lo", [P, 2, D], F32R)
        y = sb("y", [P, KT, T], F32)
        yh = sb("yh", [P, 2, KT, T], F32R)
        yl = sb("yl", [P, 2, KT, T], F32R)
        s_act = sb("s_act", [P, 2, T], F32)
        h = sb("h", [P, 2, T], F32)
        hh = sb("hh", [P, 3, T], F32R)
        hl = sb("hl", [P, 3, T], F32R)
        x = sb("x", [P, KT, T], F32)
        xn = sb("xn", [P, KT, T], F32)
        g = sb("g", [P, KT, T], F32)

        ring = [pb(f"ring{i}") for i in range(4)]
        acc = [pb(f"acc{i}") for i in range(KT)]

        S_ = Signals(nc, ctx, {
            "y_loaded": 16, "tail_loaded": 48, "out_stored": 16, "yh_done": 1, "yl_done": 1,
            "swi_hi": NJ, "swi_lo": NJ, "out_hi": NJ, "out_lo": NJ,
            "u_mm": NJ, "g_mm": NJ, "s_done": NJ, "h_done": NJ, "hh_done": NJ, "hl_done": NJ,
            "down_done": NJ, "acc_read": KT, "gated": 1, "base_done": 1, "out_ready": KT,
        }, "b_")
        swi_in = [sem(f"swi_in{j}") for j in range(NJ)]
        out_in = [sem(f"out_in{j}") for j in range(NJ)]

        block = ctx.enter_context(nc.Block())

        @block.sync
        def _(sp):
            sp.dma_start(y[:, :, :], y_d[0]).then_inc(S_["y_loaded"], 16)
            for j in range(NJ):
                sp.dma_start(swi[:, j, :], wswi_d[j]).then_inc(swi_in[j], 16)
                sp.dma_start(wout[:, j, :], wout_d[j]).then_inc(out_in[j], 16)

            def chunk(c, nxt):
                S_.await_(sp, "yh_done", c, 1)
                S_.await_(sp, "yl_done", c, 1)
                sp.dma_start(y[:, :, :], y_d[bass.ds(nxt, 1)].rearrange("c p k t -> p (c k) t"))\
                    .then_inc(S_["y_loaded"], 16)
                S_.await_(sp, "out_stored", c, 0)
                for dst, src in ((xn, xn_d), (g, g_d), (x, x_d)):
                    sp.dma_start(dst[:, :, :], src[bass.ds(c, 1)].rearrange("c p k t -> p (c k) t"))\
                        .then_inc(S_["tail_loaded"], 16)
                S_.await_(sp, "out_ready", c, KT)
                sp.dma_start(out_d[bass.ds(c, 1)].rearrange("c p k t -> p (c k) t"), xn[:, :, :])\
                    .then_inc(S_["out_stored"], 16)

            for half in range(HALVES):
                chunk(half, half + 1)
            with sp.Fori(1, B) as b:
                for half in range(HALVES):
                    c = b * HALVES + half
                    chunk(c, c + 1 if half + 1 < HALVES else (c + 1) % CHUNKS)
            sp.wait_ge(S_["y_loaded"], 16 * (CHUNKS + 1))
            sp.wait_ge(S_["out_stored"], 16 * CHUNKS)

        @block.gpsimd
        def _(pool):
            def chunk(c):
                S_.await_(pool, "tail_loaded", c, 48)
                pool.tensor_tensor(xn[:, :, :], xn[:, :, :], g[:, :, :], ALU.mult).then_inc(S_["gated"], 1)
                S_.await_(pool, "gated", c, 1)
                pool.tensor_tensor(x[:, :, :], xn[:, :, :], x[:, :, :], ALU.add).then_inc(S_["base_done"], 1)

            for half in range(HALVES):
                chunk(half)
            with pool.Fori(1, B) as b:
                for half in range(HALVES):
                    chunk(b * HALVES + half)

        @block.scalar
        def _(act):
            def split_swi(c, j):
                S_.await_(act, "g_mm", c, j - 1)
                act.activation(swi_hi[:, j % 2, :], swi[:, j % NJ, :], ACT.Copy).then_inc(S_["swi_hi"], 1)

            def split_out(c, j):
                S_.await_(act, "down_done", c, j - 1)
                act.activation(out_hi[:, j % 2, :], wout[:, j, :], ACT.Copy).then_inc(S_["out_hi"], 1)

            def high_y(c, slot):
                S_.await_(act, "y_loaded", c + 1, 16)
                S_.await_(act, "g_mm", c, 0)
                act.activation(yh[:, slot, :, :], y[:, :, :], ACT.Copy).then_inc(S_["yh_done"], 1)

            act.preload_act_table(ACT.Silu)
            high_y(-1, 0)
            act.wait_ge(swi_in[0], 16)
            split_swi(0, 0)

            def chunk(c, half, first):
                for j in range(NJ + 1):
                    if j < NJ:
                        if first and j + 1 < NJ:
                            act.wait_ge(swi_in[j + 1], 16)
                        split_swi(c, j + 1)
                        S_.await_(act, "u_mm", c, j + 1)
                        S_.await_(act, "h_done", c, j - 1)
                        act.activation(s_act[:, j % 2, :], ring[2 * j % 4][:, :], ACT.Silu)\
                            .then_inc(S_["s_done"], 1)
                    if j >= 1:
                        i = j - 1
                        S_.await_(act, "h_done", c, i + 1)
                        S_.await_(act, "down_done", c, i - 2)
                        act.activation(hh[:, i % 3, :], h[:, i % 2, :], ACT.Copy).then_inc(S_["hh_done"], 1)
                        if first:
                            act.wait_ge(out_in[i], 16)
                        split_out(c, i)
                    if j == 8:
                        high_y(c, 1 - half)

            for half in range(HALVES):
                chunk(half, half, half == 0)
            with act.Fori(1, B) as b:
                for half in range(HALVES):
                    chunk(b * HALVES + half, half, False)

        @block.vector
        def _(dve):
            def rest_swi(c, j):
                S_.await_(dve, "swi_hi", c, j + 1)
                S_.await_(dve, "g_mm", c, j - 1)
                dve.tensor_tensor(swi_lo[:, j % 2, :], swi[:, j % NJ, :], swi_hi[:, j % 2, :].bitcast(F32),
                                  ALU.subtract).then_inc(S_["swi_lo"], 1)

            def rest_out(c, j):
                S_.await_(dve, "out_hi", c, j + 1)
                S_.await_(dve, "down_done", c, j - 1)
                dve.tensor_tensor(out_lo[:, j % 2, :], wout[:, j, :], out_hi[:, j % 2, :].bitcast(F32),
                                  ALU.subtract).then_inc(S_["out_lo"], 1)

            def rest_y(c, slot):
                S_.await_(dve, "yh_done", c + 1, 1)
                dve.tensor_tensor(yl[:, slot, :, :], y[:, :, :], yh[:, slot, :, :].bitcast(F32),
                                  ALU.subtract).then_inc(S_["yl_done"], 1)

            rest_y(-1, 0)
            rest_swi(0, 0)

            def chunk(c, half):
                for j in range(NJ + 1):
                    if j < NJ:
                        rest_swi(c, j + 1)
                        S_.await_(dve, "s_done", c, j + 1)
                        S_.await_(dve, "g_mm", c, j + 1)
                        S_.await_(dve, "hh_done", c, j - 1)
                        S_.await_(dve, "hl_done", c, j - 1)
                        dve.tensor_tensor(h[:, j % 2, :], s_act[:, j % 2, :], ring[(2 * j + 1) % 4][:, :],
                                          ALU.mult).then_inc(S_["h_done"], 1)
                    if j >= 1:
                        i = j - 1
                        S_.await_(dve, "hh_done", c, i + 1)
                        S_.await_(dve, "down_done", c, i - 2)
                        dve.tensor_tensor(hl[:, i % 3, :], h[:, i % 2, :], hh[:, i % 3, :].bitcast(F32),
                                          ALU.subtract).then_inc(S_["hl_done"], 1)
                        rest_out(c, i)
                    if j == 8:
                        rest_y(c, 1 - half)
                S_.await_(dve, "down_done", c, NJ)
                S_.await_(dve, "base_done", c, 1)
                for t in range(KT):
                    dve.tensor_tensor(g[:, t, :], g[:, t, :], acc[t][:, :], ALU.mult)\
                        .then_inc(S_["acc_read"], 1)
                    S_.await_(dve, "acc_read", c, t + 1)
                    dve.tensor_tensor(xn[:, t, :], g[:, t, :], x[:, t, :], ALU.add)\
                        .then_inc(S_["out_ready"], 1)

            for half in range(HALVES):
                chunk(half, half)
            with dve.Fori(1, B) as b:
                for half in range(HALVES):
                    chunk(b * HALVES + half, half)

        @block.tensor
        def _(pe):
            def chunk(c, half):
                S_.await_(pe, "yh_done", c, 1)
                S_.await_(pe, "yl_done", c, 1)
                for j in range(NJ + LAG):
                    if j < NJ:
                        S_.await_(pe, "swi_hi", c, j + 1)
                        S_.await_(pe, "swi_lo", c, j + 1)
                        for which in range(2):
                            S_.await_(pe, ("s_done", "h_done")[which], c, j - 1)
                            i = 0
                            for k in range(KT):
                                col = ((1 - which) * KT + k) * P
                                for w, a in ((swi_hi, yh), (swi_hi, yl), (swi_lo, yh)):
                                    last = pe.matmul(ring[(2 * j + which) % 4][:, :], w[:, j % 2, col:col + P],
                                                     a[:, half, k, :], start=(i == 0), stop=(i == 3 * KT - 1))
                                    i += 1
                            last.then_inc(S_[("u_mm", "g_mm")[which]], 1)
                    if j >= LAG:
                        i = j - LAG
                        S_.await_(pe, "hl_done", c, i + 1)
                        S_.await_(pe, "out_lo", c, i + 1)
                        if i == 0:
                            S_.await_(pe, "acc_read", c, 0)
                        for t in range(KT):
                            n = 0
                            for w, a in ((out_hi, hh), (out_hi, hl), (out_lo, hh)):
                                last = pe.matmul(acc[t][:, :], w[:, i % 2, t * P:(t + 1) * P], a[:, i % 3, :],
                                                 start=(i == 0 and n == 0), stop=(i == NJ - 1 and n == 2))
                                n += 1
                        last.then_inc(S_["down_done"], 1)

            for half in range(HALVES):
                chunk(half, half)
            with pe.Fori(1, B) as b:
                for half in range(HALVES):
                    chunk(b * HALVES + half, half)


def build(nc, x_d, wqkv_d, wswi_d, wout_d, up_d, gate_d, down_d, out_d):
    shape = (CHUNKS, P, KT, T)
    xn_d, y_d, g_d = (nc.dram_tensor(n, shape, F32, kind="Internal").ap() for n in ("xn_dram", "y_dram", "g_dram"))
    phase_a(nc, x_d, wqkv_d, (up_d, gate_d, down_d), xn_d, y_d, g_d)
    phase_b(nc, x_d, wswi_d, wout_d, xn_d, y_d, g_d, out_d)


def kernel(**inputs):
    import numpy as np
    import concourse.bacc as bacc
    from concourse.bass_utils import run_bass_kernel_spmd as run

    def a(name):
        return np.ascontiguousarray(inputs[name])

    def lay(v):
        return np.ascontiguousarray(v)

    x = lay(a("L0_attn_x").reshape(CHUNKS, T, KT, P).transpose(0, 3, 2, 1))
    wqkv = lay(a("L0_attn_w_qkv").reshape(4, 3, P, KT, P).transpose(0, 4, 1, 3, 2)).reshape(4, P, 3 * KT * P)
    wswi = lay(a("L0_attn_w_swiglu").reshape(2, NJ, P, KT, P).transpose(1, 4, 0, 3, 2)).reshape(NJ, P, 2 * KT * P)
    wout = lay(a("L0_attn_w_out").reshape(D, NJ, P).transpose(1, 2, 0))
    up, gate = (lay(a(n).reshape(NJ // 2, 2, P, KT, P).transpose(0, 4, 1, 3, 2)).reshape(NJ // 2, P, 2 * KT * P)
                for n in ("L0_ffn_W_up", "L0_ffn_W_gate"))
    down = lay(a("L0_ffn_W_down").reshape(D, NJ // 2, 2, P).transpose(1, 3, 2, 0)).reshape(NJ // 2, P, 2 * D)

    nc = bacc.Bacc("TRN2", target_bir_lowering=False, num_devices=1)
    arrays = {"x": x, "wqkv": wqkv, "wswi": wswi, "wout": wout, "up": up, "gate": gate, "down": down}
    args = [nc.dram_tensor("in_" + n, v.shape, F32, kind="ExternalInput").ap() for n, v in arrays.items()]
    out = nc.dram_tensor("out_x", (CHUNKS, P, KT, T), F32, kind="ExternalOutput").ap()
    build(nc, *args, out)
    r = run(nc, [{"in_" + n: v for n, v in arrays.items()}], core_ids=[0])
    got = r.results[0]["out_x"]
    return lay(got.transpose(0, 3, 2, 1)).reshape(B, S, D)
```

```python
from contextlib import ExitStack

import concourse.bass as bass
from concourse import mybir

F32 = mybir.dt.float32
F32R = mybir.dt.float32r
F16 = mybir.dt.float16
U32 = mybir.dt.uint32
ALU = mybir.AluOpType
ACT = mybir.ActivationFunctionType
AX = mybir.AxisListType
RMAX = bass.bass_isa.ReduceOp.max

P = 128
B, S, D = 4, 1024, 512
E = 2048
T = 512
HALVES = S // T
CHUNKS = B * HALVES
KT = D // P
NJ = E // P
M3 = 3 * KT
LN_EPS = 1e-5
RMS_EPS = 1.1920929e-07
QUANT_EPS = 1e-8
DEN_EPS = 1e-6
LAG = 2
GRAN = 256
PER_T = T // GRAN

XS = 2.0 ** 10
HS = 2.0 ** -14
TERN = (1.0, 2.0, 2.0)
WTOP = 2.0 ** 14

QKV_ORDER = list(range(KT, 2 * KT)) + list(range(0, KT)) + list(range(2 * KT, 3 * KT))
K0, Q0, V0 = 0, KT, 2 * KT
UNIT = 2 * KT * P

WQ_ORDER = (1, 2, 0, 3)
WQ = M3 * D // 4
PIECE = 1024
PAIRS = NJ // 2
STAGES = 4
PIECES = [(m, g) for g in range(PAIRS) for m in range(3)]
FIRST = 12
SUMS = PIECES[STAGES:STAGES + FIRST] + PIECES[:STAGES] + PIECES[STAGES + FIRST:]
DVE_SUMS = list(range(1, len(SUMS) - 2, 3))
ACT_SUMS = [n for n in range(len(SUMS)) if n not in DVE_SUMS]
SLOT_OF = [-1, -1, -1, -1, 0, 1] + [2 * g - 3 + m for g in range(2, PAIRS) for m in range(3)]
QUANT_AT = {j: [n for n, at in enumerate(SLOT_OF) if at == j] for j in range(-1, NJ)}

ARENA_KIB = 206


class Signals:

    def __init__(self, nc, ctx, prefix, per_chunk):
        self.per = per_chunk
        self.sem = {n: ctx.enter_context(nc.semaphore(prefix + n)) for n in per_chunk}

    def __getitem__(self, name):
        return self.sem[name]

    def wait(self, eng, name, c, k):
        v = c * self.per[name] + k
        if isinstance(v, int) and v <= 0:
            return
        eng.wait_ge(self.sem[name], v)


def each_chunk(eng, chunk):
    for half in range(HALVES):
        chunk(half, half)
    with eng.Fori(1, B - 1) as b:
        for half in range(HALVES):
            chunk(b * HALVES + half, half)
    for half in range(HALVES):
        chunk((B - 1) * HALVES + half, half)


def is_first(c):
    return isinstance(c, int) and c == 0


def is_last(c):
    return isinstance(c, int) and c == CHUNKS - 1


def build(nc, x_d, wqkv_d, wswi_d, wout_d, up_d, gate_d, down_d, out_d):
    shape = (CHUNKS, P, KT, T)
    xn_d, y_d, g_d = (nc.dram_tensor(n, shape, F32, kind="Internal").ap() for n in ("xn_dram", "y_dram", "g_dram"))
    ternary_d = (up_d, gate_d, down_d)
    LAST = CHUNKS - 1

    with ExitStack() as ctx:
        start = (nc.sbuf_base + 31) // 32 * 32
        ctx.enter_context(nc.sbuf_tensor("arena", [P, ARENA_KIB * 1024], mybir.dt.uint8))

        def place(name, offset, shape, dt):
            return nc.alloc_sbuf_tensor_at(name, shape, dt, offset=start + offset * 1024)

        wq_hi = place("wq_hi", 0, [P, M3, KT, P], F16)
        wq_lo = place("wq_lo", 12, [P, M3, KT, P], F16)
        tern = [place(n, 24 + 16 * i, [P, NJ * KT * P], F16)
                for i, n in enumerate(("tern_up", "tern_gate", "tern_down"))]
        first = place("first", 24, [P, FIRST, PIECE], F32)
        xh = place("xh", 72, [P, 2, KT, T], F16)
        xl = place("xl", 80, [P, 2, KT, T], F16)
        kqv = place("kqv", 88, [P, M3, T], F32)
        sq = place("sq", 112, [P, KT, T], F32)
        add2 = place("add2", 120, [P, 2, T], F32)
        var2 = place("var2", 124, [P, 2, T], F32)
        x = place("x", 128, [P, KT, T], F32)
        inv2 = place("inv2", 136, [P, 2, T], F32)
        r_t = place("r_t", 140, [P, T], F32)
        m2 = place("m2", 142, [P, T], F32)
        kq_ms = place("kq_ms", 144, [P, 2, T], F32)
        hh = place("hh", 148, [P, 3, T], F16)
        hl = place("hl", 151, [P, 3, T], F16)
        g_out = place("g_out", 156, [P, KT, T], F32)
        below = place("below", 164, [P, 2, PIECE], F16)
        add_hi = place("add_hi", 168, [P, T], F32R)
        add1 = place("add1", 170, [P, T], F32)
        stage = place("stage", 172, [P, STAGES, PIECE], F32)
        sign_hi = place("sign_hi", 188, [P, 2, PIECE], F16)
        sign_lo = place("sign_lo", 192, [P, 2, PIECE], F16)
        mean_w = place("mean_w", 196, [P, P], F32)
        count_w = place("count_w", 200, [P, P], F32)
        s_act = place("s_act", 196, [P, 2, T], F32)
        h = place("h", 200, [P, 2, T], F32)
        add_lo = place("add_lo", 204, [P, T], F32R)

        yh = [place("yh0", 0, [P, KT, T], F32R), place("yh1", 140, [P, KT, T], F32R)]
        yl = [place("yl0", 8, [P, KT, T], F32R), place("yl1", 148, [P, KT, T], F32R)]
        swi_hi = [place("swi_hi0", 16, [P, UNIT], F32R), place("swi_hi1", 112, [P, UNIT], F32R)]
        swi_lo = [place("swi_lo0", 20, [P, UNIT], F32R), place("swi_lo1", 116, [P, UNIT], F32R)]
        swi_head = place("swi_head", 172, [P, 4, UNIT], F32)
        swi_rest = place("swi_rest", 24, [P, NJ - 4, UNIT], F32)
        wout = [place("wout0", 72, [P, 8, D], F32), place("wout1", 88, [P, 8, D], F32)]
        xb = place("xb", 104, [P, KT, T], F32)
        out_hi = place("out_hi", 120, [P, 2, D], F32R)
        out_lo = place("out_lo", 124, [P, 2, D], F32R)
        hhb = place("hhb", 128, [P, 3, T], F32R)
        hlb = place("hlb", 134, [P, 3, T], F32R)
        gb = place("gb", 156, [P, KT, T], F32)
        xnb = place("xnb", 164, [P, KT, T], F32)
        yb = place("yb", 188, [P, KT, T], F32)

        def swi(j):
            return swi_head[:, j, :] if j < 4 else swi_rest[:, j - 4, :]

        def w_out(j):
            return wout[j // 8][:, j % 8, :]

        def sb(name, shape, dt=F32):
            return ctx.enter_context(nc.sbuf_tensor(name, shape, dt))

        def sem(name):
            return ctx.enter_context(nc.semaphore(name))

        mean_r = sb("mean_r", [P, P], F32R)
        one_col = sb("one_col", [P, 1])
        carry = sb("carry", [P, 2, KT])
        absum = sb("absum", [P, 3, PAIRS])
        absum3 = sb("absum3", [P, 3])
        scale3 = sb("scale3", [P, 3])
        half3 = sb("half3", [P, 3])
        nhalf3 = sb("nhalf3", [P, 3])
        c_up = sb("c_up", [P, 1])
        inv_up = sb("inv_up", [P, 2])
        c_ffn = sb("c_ffn", [P, 3])
        wmax = sb("wmax", [P, 2])
        bound = sb("bound", [P, 2])
        wsum = sb("wsum", [P, 3])
        wpow = sb("wpow", [P, 2])
        inv_w = sb("inv_w", [P, 2])
        s_w = sb("s_w", [P, 2])
        c_w = sb("c_w", [P, 2])

        ring = [ctx.enter_context(nc.psum_tensor(f"ring{i}", [P, T], F32)) for i in range(4)]
        acc = [ctx.enter_context(nc.psum_tensor(f"acc{i}", [P, T], F32)) for i in range(KT)]
        stat = ring[3]
        stat0 = ring[2]

        SA = Signals(nc, ctx, "a_", {
            "x_loaded": 16, "xn_stored": 16, "y_stored": 16, "g_stored": 16,
            "fold_half": 4, "fold_done": 12, "stat_mm": 4, "stat_read": 4, "sq_done": 3,
            "centred": 1, "var_root": 1, "inv_x": 2 * PER_T, "norms": 3, "xh_done": 1, "xl_done": 1,
            "qkv_mm": M3, "qkv_read": M3, "kq_root": 1, "inv_kq": 2 * PER_T, "kq_scaled": 2 * KT,
            "exped": 2, "wv_done": KT, "summed": 2 * KT + 2, "den_done": 1, "inv_den": KT * PER_T,
            "y_done": KT, "u_mm": NJ, "g_mm": NJ, "s_done": NJ, "h_done": NJ, "hh_done": NJ, "hl_done": NJ,
            "down_done": NJ, "g_act": KT,
        })
        SB = Signals(nc, ctx, "b_", {
            "y_loaded": 16, "tail_loaded": 48, "out_stored": 16 * KT, "yh_done": 1, "yl_done": 1,
            "swi_hi": NJ, "swi_lo": NJ, "out_hi": NJ, "out_lo": NJ,
            "u_mm": NJ, "g_mm": NJ, "s_done": NJ, "h_done": NJ, "hh_done": NJ, "hl_done": NJ,
            "down_done": NJ, "acc_read": KT, "gated": 1, "base_done": 1, "out_ready": KT,
        })
        wq_in = [sem(f"wq_in{i}") for i in range(4)]
        first_in = [sem(f"first_in{i}") for i in range(FIRST)]
        stage_in = [sem(f"stage_in{i}") for i in range(STAGES)]
        swi_in = [sem(f"swi_in{j}") for j in range(NJ)]
        out_in = [sem(f"out_in{j}") for j in range(NJ)]
        consts = sem("consts")
        x0_in = [sem(f"x0_in{k}") for k in range(KT)]
        x0_centred = sem("x0_centred")
        x0_squared = sem("x0_squared")
        x0_norm = sem("x0_norm")
        x0_high = sem("x0_high")
        x0_low = sem("x0_low")
        acc_last = sem("acc_last")
        wsum_s = sem("wsum_done")
        wmax_s = sem("wmax_done")
        wmax_all = sem("wmax_all")
        wscale = sem("wscale")
        wq_hi_s = sem("wq_hi_done")
        wq_lo_s = sem("wq_lo_done")
        wq_last_s = sem("wq_last")
        absact_s = sem("absact")
        absdve_s = sem("absdve")
        absum_s = sem("absum_done")
        mean3_s = sem("mean3")
        scales_s = sem("scales")
        below_s = sem("below_done")
        below0_s = sem("below0_done")
        signs_s = sem("signs")
        tern_s = sem("tern")

        wq_raw_f = kqv[:, :, :].rearrange("p a b -> p (a b)")

        def wq_raw(n):
            return wq_raw_f[:, n * WQ:(n + 1) * WQ]

        wq_hi_f = wq_hi[:, :, :, :].rearrange("p a b c -> p (a b c)")
        wq_lo_f = wq_lo[:, :, :, :].rearrange("p a b c -> p (a b c)")
        up = tern[0][:, :].rearrange("p (j k m) -> p j k m", j=NJ, k=KT)
        gate = tern[1][:, :].rearrange("p (j k m) -> p j k m", j=NJ, k=KT)
        down = tern[2][:, :].rearrange("p (j n) -> p j n", j=NJ)

        def piece_in(eng, n):
            eng.wait_ge(stage_in[n % STAGES], 16 * (n // STAGES + 1))

        def wq_split(eng, n):
            eng.wait_ge(*((wq_lo_s, n + 1) if n < 3 else (wq_last_s, 2)))

        def sum_piece(n):
            if FIRST <= n < FIRST + STAGES:
                return stage[:, n - FIRST, :], stage_in[n - FIRST], 16
            if n < FIRST:
                return first[:, n, :], first_in[n], 16
            return first[:, n - FIRST - STAGES, :], first_in[n - FIRST - STAGES], 32

        def wide(t):
            return t.unsqueeze(1).to_broadcast([P, KT, T])

        def chunk_of(d, c):
            return d[bass.ds(c, 1)].rearrange("c p k t -> p (c k) t")

        block = ctx.enter_context(nc.Block())

        @block.sync
        def _(sp):
            for k in range(KT):
                sp.dma_start(x[:, k, :], x_d[0][:, k, :]).then_inc(x0_in[k], 16)
            for n, i in enumerate(WQ_ORDER):
                sp.dma_start(wq_raw(n), wqkv_d[i]).then_inc(wq_in[n], 16)

            def first_pass():
                for n, (m, g) in enumerate(SUMS):
                    before = n - FIRST - STAGES
                    if before >= 0:
                        if before in ACT_SUMS:
                            sp.wait_ge(absact_s, ACT_SUMS.index(before) + 1)
                        else:
                            sp.wait_ge(absdve_s, DVE_SUMS.index(before) + 1)
                    dst, come, _ = sum_piece(n)
                    sp.dma_start(dst, ternary_d[m][g]).then_inc(come, 16)

            def second_pass():
                for n in range(STAGES, len(PIECES)):
                    m, g = PIECES[n]
                    sp.wait_ge(tern_s, n - STAGES + 1)
                    sp.dma_start(stage[:, n % STAGES, :], ternary_d[m][g]).then_inc(stage_in[n % STAGES], 16)

            def load_swi(j):
                sp.dma_start(swi(j), wswi_d[j]).then_inc(swi_in[j], 16)

            def load_out(j):
                sp.dma_start(w_out(j), wout_d[j]).then_inc(out_in[j], 16)

            def chunk(c, half):
                if is_first(c):
                    first_pass()
                SA.wait(sp, "norms", c, 1)
                sp.dma_start(chunk_of(xn_d, c), x[:, :, :]).then_inc(SA["xn_stored"], 16)
                if not is_last(c):
                    SA.wait(sp, "xh_done", c, 1)
                    SA.wait(sp, "xl_done", c, 1)
                    SA.wait(sp, "xn_stored", c, 16)
                    sp.dma_start(x[:, :, :], chunk_of(x_d, c + 1)).then_inc(SA["x_loaded"], 16)
                if is_first(c):
                    second_pass()
                if is_last(c):
                    sp.wait_ge(tern_s, len(PIECES))
                    sp.wait_ge(SA["y_stored"], 16)
                    sp.dma_start(yb[:, :, :], y_d[0]).then_inc(SB["y_loaded"], 16)
                    for j in range(4):
                        load_swi(j)
                    SA.wait(sp, "g_mm", c, NJ)
                    for j in range(2):
                        load_out(j)
                        load_swi(4 + j)
                SA.wait(sp, "y_done", c, KT)
                sp.dma_start(chunk_of(y_d, c), kqv[:, V0:V0 + KT, :]).then_inc(SA["y_stored"], 16)
                if is_last(c):
                    for j in range(2, 8):
                        load_out(j)
                        load_swi(4 + j)
                SA.wait(sp, "g_act", c, KT)
                sp.dma_start(chunk_of(g_d, c), g_out[:, :, :]).then_inc(SA["g_stored"], 16)

            each_chunk(sp, chunk)
            for j in range(8, NJ):
                if j + 4 < NJ:
                    load_swi(j + 4)
                load_out(j)
            for name in ("xn_stored", "y_stored", "g_stored"):
                sp.wait_ge(SA[name], 16 * CHUNKS)
            sp.wait_ge(SA["stat_mm"], 4 * CHUNKS)

            def attend(c, half):
                if not is_last(c):
                    SB.wait(sp, "yh_done", c, 1)
                    SB.wait(sp, "yl_done", c, 1)
                    sp.dma_start(yb[:, :, :], chunk_of(y_d, c + 1)).then_inc(SB["y_loaded"], 16)
                SB.wait(sp, "out_stored", c, 0)
                for dst, src in ((xnb, xn_d), (gb, g_d), (xb, x_d)):
                    sp.dma_start(dst[:, :, :], chunk_of(src, c)).then_inc(SB["tail_loaded"], 16)
                for t in range(KT):
                    SB.wait(sp, "out_ready", c, t + 1)
                    sp.dma_start(chunk_of(out_d, c)[:, t, :], xnb[:, t, :]).then_inc(SB["out_stored"], 16)

            each_chunk(sp, attend)
            sp.wait_ge(SB["out_stored"], 16 * KT * CHUNKS)

        @block.gpsimd
        def _(pool):
            pool.memset(mean_w[:, :], 1.0 / D).then_inc(consts, 1)
            pool.memset(count_w[:, :], 1.0 / (E * D)).then_inc(consts, 1)
            pool.memset(one_col[:, :], 1.0).then_inc(consts, 1)
            pool.wait_ge(consts, 3)
            pool.tensor_copy(mean_r[:, :], mean_w[:, :]).then_inc(consts, 1)
            pool.wait_ge(wmax_s, 1)
            pool.partition_all_reduce(bound[:, 0:1], wmax[:, 0:1], P, RMAX).then_inc(wmax_all, 1)
            pool.wait_ge(wmax_s, 2)
            pool.partition_all_reduce(bound[:, 1:2], wmax[:, 1:2], P, RMAX).then_inc(wmax_all, 1)

            pool.wait_ge(wscale, 10)
            pool.wait_ge(wq_hi_s, 4)
            pool.tensor_scalar(wq_raw(3), wq_raw(3), s_w[:, 1:2], None, ALU.mult).then_inc(wq_last_s, 1)
            pool.wait_ge(wq_last_s, 1)
            cols = slice(WQ_ORDER[3] * WQ, (WQ_ORDER[3] + 1) * WQ)
            pool.tensor_tensor(wq_lo_f[:, cols], wq_raw(3), wq_hi_f[:, cols], ALU.subtract).then_inc(wq_last_s, 1)

            def fold(c, k, src):
                SA.wait(pool, "stat_mm", c, k - 1)
                SA.wait(pool, "fold_done", c, 3 * (k - 3))
                pool.tensor_tensor(add2[:, :, :], src[:, 0:2, :], src[:, 2:4, :], ALU.add)\
                    .then_inc(SA["fold_half"], 1)
                SA.wait(pool, "fold_half", c, k - 2)
                pool.tensor_tensor(add1[:, :], add2[:, 0, :], add2[:, 1, :], ALU.add)\
                    .then_inc(SA["fold_done"], 1)
                pool.tensor_tensor(add_hi[:, :], add2[:, 0, :], add2[:, 1, :], ALU.add)\
                    .then_inc(SA["fold_done"], 1)
                SA.wait(pool, "fold_done", c, 3 * (k - 3) + 2)
                pool.tensor_tensor(add_lo[:, :], add1[:, :], add_hi[:, :].bitcast(F32), ALU.subtract)\
                    .then_inc(SA["fold_done"], 1)

            def below_half(n):
                g = n // 3
                piece_in(pool, n)
                if g >= 2:
                    pool.wait_ge(tern_s, 3 * (g - 2) + 1)
                pool.tensor_scalar(below[:, g % 2, :], stage[:, n % STAGES, :], nhalf3[:, 0:1], None, ALU.is_lt)\
                    .then_inc(below_s, 1)

            def chunk(c, half):
                SA.wait(pool, "sq_done", c, 2)
                fold(c, 3, sq)
                SA.wait(pool, "sq_done", c, 3)
                fold(c, 4, sq)
                if is_first(c):
                    pool.wait_ge(scales_s, 6)
                    below_half(3)
                if not is_last(c):
                    SA.wait(pool, "x_loaded", c, 16)
                    fold(c, 5, x)

                def scale_kq(t):
                    which = t // KT
                    SA.wait(pool, "inv_kq", c, (which + 1) * PER_T)
                    pool.tensor_tensor(kqv[:, t, :], kqv[:, t, :], kq_ms[:, which, :], ALU.mult)\
                        .then_inc(SA["kq_scaled"], 1)

                def wv(t):
                    SA.wait(pool, "exped", c, 1)
                    pool.tensor_tensor(kqv[:, V0 + t, :], kqv[:, V0 + t, :], kqv[:, K0 + t, :], ALU.mult)\
                        .then_inc(SA["wv_done"], 1)

                def y(t):
                    SA.wait(pool, "inv_den", c, (t + 1) * PER_T)
                    pool.tensor_tensor(kqv[:, V0 + t, :], kqv[:, V0 + t, :], kqv[:, Q0 + t, :], ALU.mult)\
                        .then_inc(SA["y_done"], 1)

                def fold_squares():
                    SA.wait(pool, "sq_done", c, 4)
                    fold(c, 6, sq)

                jobs = {1: [(scale_kq, 0), (scale_kq, 1)], 2: [(scale_kq, 2), (scale_kq, 3)],
                        3: [(scale_kq, 4), (scale_kq, 5)], 4: [(scale_kq, 6), (scale_kq, 7)],
                        5: [(wv, 0), (wv, 1)], 6: [(wv, 2), (wv, 3)]}
                if is_last(c):
                    jobs |= {13: [(y, 0)], 14: [(y, 1)], 15: [(y, 2)], 16: [(y, 3)]}
                else:
                    jobs |= {8 if is_first(c) else 7: [(fold_squares,)], 16: [(y, 0), (y, 1), (y, 2), (y, 3)]}
                for j in range(NJ + 1):
                    if j >= 1:
                        i = j - 1
                        SA.wait(pool, "hh_done", c, i + 1)
                        SA.wait(pool, "down_done", c, i - 2)
                        pool.tensor_tensor(hl[:, i % 3, :], h[:, i % 2, :], hh[:, i % 3, :], ALU.subtract)\
                            .then_inc(SA["hl_done"], 1)
                    for job in jobs.get(j, []):
                        job[0](*job[1:])
                    if is_first(c):
                        for n in QUANT_AT.get(j, ()):
                            if n > 3 and n % 3 == 0:
                                below_half(n)

            each_chunk(pool, chunk)

            def attend(c, half):
                SB.wait(pool, "tail_loaded", c, 48)
                pool.tensor_tensor(xnb[:, :, :], xnb[:, :, :], gb[:, :, :], ALU.mult).then_inc(SB["gated"], 1)
                SB.wait(pool, "gated", c, 1)
                pool.tensor_tensor(xb[:, :, :], xnb[:, :, :], xb[:, :, :], ALU.add).then_inc(SB["base_done"], 1)

            each_chunk(pool, attend)

        @block.scalar
        def _(act):
            def roots(c):
                SA.wait(act, "stat_read", c, 6)
                act.activation(var2[:, :, :], var2[:, :, :], ACT.Sqrt).then_inc(SA["var_root"], 1)

            def square_x(c):
                SA.wait(act, "centred", c + 1, 1)
                SA.wait(act, "fold_half", c, 2)
                act.activation(sq[:, :, :], x[:, :, :], ACT.Square).then_inc(SA["sq_done"], 1)

            def high_x(c, slot):
                SA.wait(act, "norms", c + 1, 1)
                SA.wait(act, "g_mm", c, 0)
                act.activation(xh[:, slot, :, :], x[:, :, :], ACT.Copy, scale=XS).then_inc(SA["xh_done"], 1)

            def split_wq(n):
                i = WQ_ORDER[n]
                group = min(n, 1)
                act.wait_ge(wscale, 5 * group + 4)
                act.activation(wq_hi_f[:, i * WQ:(i + 1) * WQ], wq_raw(n), ACT.Copy,
                               scale=s_w[:, group:group + 1]).then_inc(wq_hi_s, 1)

            below_f = below[:, :, :].rearrange("p a b -> p (a b)")

            def bound_wq(n):
                act.wait_ge(wq_in[n], 16)
                if n >= 2:
                    act.wait_ge(wsum_s, n - 1)
                act.activation(below_f[:, 0:WQ], wq_raw(n), ACT.Abs,
                               accum_out=wsum[:, n - 1:n]).then_inc(wsum_s, 1)

            def abs_sum(n):
                (m, g), (src, come, value) = SUMS[n], sum_piece(n)
                done = ACT_SUMS.index(n)
                act.wait_ge(come, value)
                if done == 0:
                    act.wait_ge(wsum_s, 3)
                if done >= 2:
                    act.wait_ge(absact_s, done - 1)
                act.activation(below[:, done % 2, :], src, ACT.Abs, accum_out=absum[:, m, g:g + 1])\
                    .then_inc(absact_s, 1)

            def signs(n):
                g, m = divmod(n, 3)
                if m == 0:
                    return
                i = 2 * g + m - 1
                piece_in(act, n)
                if g >= 1:
                    act.wait_ge(tern_s, n - 2)
                act.activation(sign_hi[:, i % 2, :], stage[:, n % STAGES, :], ACT.Sign,
                               bias=nhalf3[:, m:m + 1], scale=1.0 - 2.0 ** -24)
                act.activation(sign_lo[:, i % 2, :], stage[:, n % STAGES, :], ACT.Sign,
                               bias=half3[:, m:m + 1], scale=1.0 - 2.0 ** -24).then_inc(signs_s, 1)

            def split_swi(c, j):
                SB.wait(act, "g_mm", c, j - 1)
                act.activation(swi_hi[j % 2][:, :], swi(j % NJ), ACT.Copy).then_inc(SB["swi_hi"], 1)

            def split_out(c, j):
                SB.wait(act, "down_done", c, j - 1)
                act.activation(out_hi[:, j % 2, :], w_out(j), ACT.Copy).then_inc(SB["out_hi"], 1)

            def high_y(c, slot):
                SB.wait(act, "y_loaded", c + 1, 16)
                SB.wait(act, "g_mm", c, 0)
                act.activation(yh[slot][:, :, :], yb[:, :, :], ACT.Copy).then_inc(SB["yh_done"], 1)

            def first_y():
                SA.wait(act, "qkv_mm", LAST, M3)
                high_y(-1, 0)

            def first_swi():
                act.wait_ge(swi_in[0], 16)
                split_swi(0, 0)
                SA.wait(act, "fold_half", LAST, 2)
                act.wait_ge(swi_in[1], 16)
                split_swi(0, 1)

            for k in range(KT):
                act.wait_ge(x0_centred, k + 1)
                act.activation(sq[:, k, :], x[:, k, :], ACT.Square).then_inc(x0_squared, 1)
            act.wait_ge(x0_squared, KT)
            act.sem_inc(SA["sq_done"], 1)
            bound_wq(1)
            roots(-1)
            split_wq(0)
            bound_wq(2)
            bound_wq(3)
            for k in range(KT):
                act.wait_ge(x0_norm, k + 1)
                act.activation(xh[:, 0, k, :], x[:, k, :], ACT.Copy, scale=XS).then_inc(x0_high, 1)
            act.wait_ge(x0_high, KT)
            act.sem_inc(SA["xh_done"], 1)
            for n in range(1, 4):
                split_wq(n)

            def chunk(c, half):
                if is_first(c):
                    for n in ACT_SUMS[:10]:
                        abs_sum(n)
                SA.wait(act, "qkv_read", c, KT)
                SA.wait(act, "fold_half", c, 0)
                act.activation(sq[:, :, :], kqv[:, K0:K0 + KT, :], ACT.Square).then_inc(SA["sq_done"], 1)
                if is_first(c):
                    for n in ACT_SUMS[10:]:
                        abs_sum(n)
                SA.wait(act, "qkv_read", c, 2 * KT)
                SA.wait(act, "fold_half", c, 1)
                act.activation(sq[:, :, :], kqv[:, Q0:Q0 + KT, :], ACT.Square).then_inc(SA["sq_done"], 1)
                if is_first(c):
                    act.wait_ge(scales_s, 6)
                    for n in QUANT_AT[-1]:
                        signs(n)

                def root_kq():
                    SA.wait(act, "stat_read", c, 4)
                    act.activation(kq_ms[:, :, :], kq_ms[:, :, :], ACT.Sqrt).then_inc(SA["kq_root"], 1)

                def exp_kq():
                    SA.wait(act, "kq_scaled", c, KT)
                    act.activation(kqv[:, K0:K0 + KT, :], kqv[:, K0:K0 + KT, :], ACT.Exp)\
                        .then_inc(SA["exped"], 1)
                    SA.wait(act, "kq_scaled", c, 2 * KT)
                    act.activation(kqv[:, Q0:Q0 + KT, :], kqv[:, Q0:Q0 + KT, :], ACT.Exp, scale=-1.0)\
                        .then_inc(SA["exped"], 1)

                jobs = {0: (root_kq,), 5: (exp_kq,)}
                if is_last(c):
                    jobs |= {8: (first_y,), 10: (first_swi,)}
                else:
                    jobs |= {4: (square_x, c), 10: (roots, c), 14: (high_x, c, 1 - half)}
                for j in range(NJ + 1):
                    if j < NJ:
                        SA.wait(act, "u_mm", c, j + 1)
                        SA.wait(act, "h_done", c, j - 1)
                        act.activation(s_act[:, j % 2, :], ring[2 * j % 3][:, :], ACT.Silu, scale=c_up[:, 0:1])\
                            .then_inc(SA["s_done"], 1)
                    if j >= 1:
                        i = j - 1
                        SA.wait(act, "h_done", c, i + 1)
                        SA.wait(act, "down_done", c, i - 2)
                        act.activation(hh[:, i % 3, :], h[:, i % 2, :], ACT.Copy).then_inc(SA["hh_done"], 1)
                    if j in jobs:
                        jobs[j][0](*jobs[j][1:])
                    if is_first(c):
                        for n in QUANT_AT.get(j, ()):
                            signs(n)
                SA.wait(act, "down_done", c, NJ)
                SA.wait(act, "g_stored", c, 0)
                for t in range(KT):
                    act.activation(g_out[:, t, :], acc[t][:, :], ACT.Silu, scale=c_ffn[:, 2:3])\
                        .then_inc(SA["g_act"], 1)

            each_chunk(act, chunk)
            SA.wait(act, "h_done", LAST, NJ)
            SA.wait(act, "hl_done", LAST, NJ)
            SA.wait(act, "xl_done", LAST, 1)
            SA.wait(act, "xn_stored", LAST, 16)
            SA.wait(act, "fold_done", LAST, 6)

            def attend(c, half):
                for j in range(NJ + 1):
                    if j >= 1 and (j + 1 < NJ or not is_last(c)):
                        if is_first(c) and j + 1 < NJ:
                            act.wait_ge(swi_in[j + 1], 16)
                        split_swi(c, j + 1)
                    if j < NJ:
                        SB.wait(act, "u_mm", c, j + 1)
                        SB.wait(act, "h_done", c, j - 1)
                        act.activation(s_act[:, j % 2, :], ring[2 * j % 4][:, :], ACT.Silu)\
                            .then_inc(SB["s_done"], 1)
                    if j >= 1:
                        i = j - 1
                        SB.wait(act, "h_done", c, i + 1)
                        SB.wait(act, "down_done", c, i - 2)
                        act.activation(hhb[:, i % 3, :], h[:, i % 2, :], ACT.Copy).then_inc(SB["hh_done"], 1)
                        if is_first(c):
                            act.wait_ge(out_in[i], 16)
                        split_out(c, i)
                    if j == 8 and not is_last(c):
                        if is_first(c):
                            SA.wait(act, "kq_scaled", LAST, 2 * KT)
                            SA.wait(act, "qkv_read", LAST, M3)
                            SA.wait(act, "stat_read", LAST, 4)
                        high_y(c, 1 - half)

            each_chunk(act, attend)

        @block.vector
        def _(dve):
            def centre(c):
                SA.wait(dve, "stat_mm", c, 5)
                SA.wait(dve, "x_loaded", c, 16)
                dve.tensor_tensor(x[:, :, :], x[:, :, :], wide(stat[:, :]), ALU.subtract)\
                    .then_inc(SA["centred"], 1)
                SA.wait(dve, "centred", c + 1, 1)
                dve.sem_inc(SA["stat_read"], 1)

            def variances(c):
                SA.wait(dve, "stat_mm", c, 6)
                SA.wait(dve, "norms", c + 1, 0)
                bank = stat0 if isinstance(c, int) and c < 0 else stat
                dve.tensor_scalar(var2[:, 0, :], bank[:, :], LN_EPS, None, ALU.add)
                dve.tensor_scalar(var2[:, 1, :], bank[:, :], 1.0 + RMS_EPS, RMS_EPS * LN_EPS,
                                  ALU.mult, ALU.add).then_inc(SA["stat_read"], 1)

            def invert_x(c, g):
                i, o = g // PER_T, g % PER_T * GRAN
                SA.wait(dve, "var_root", c + 1, 1)
                dve.reciprocal(inv2[:, i, o:o + GRAN], var2[:, i, o:o + GRAN]).then_inc(SA["inv_x"], 1)

            def normalise(c):
                SA.wait(dve, "inv_x", c + 1, PER_T)
                dve.tensor_tensor(x[:, :, :], x[:, :, :], wide(inv2[:, 0, :]), ALU.mult)\
                    .then_inc(SA["norms"], 1)

            def rms_terms(c):
                SA.wait(dve, "inv_x", c + 1, 2 * PER_T)
                dve.tensor_tensor(r_t[:, :], var2[:, 0, :], inv2[:, 1, :], ALU.mult)
                dve.tensor_tensor(m2[:, :], var2[:, 1, :], inv2[:, 0, :], ALU.mult).then_inc(SA["norms"], 1)
                SA.wait(dve, "norms", c + 1, 2)
                dve.tensor_tensor(m2[:, :], m2[:, :], m2[:, :], ALU.mult).then_inc(SA["norms"], 1)

            def low_x(c, slot):
                SA.wait(dve, "norms", c + 1, 1)
                SA.wait(dve, "xh_done", c + 1, 1)
                dve.scalar_tensor_tensor(xl[:, slot, :, :], x[:, :, :], XS, xh[:, slot, :, :],
                                         ALU.mult, ALU.subtract).then_inc(SA["xl_done"], 1)

            def scale_wq(group):
                g, done = slice(group, group + 1), 5 * group
                dve.wait_ge(wmax_all, group + 1)
                dve.tensor_scalar(wpow[:, g], bound[:, g], 1e-30, None, ALU.max).then_inc(wscale, 1)
                dve.wait_ge(wscale, done + 1)
                dve.tensor_scalar(c_w[:, g].bitcast(U32), wpow[:, g].bitcast(U32), 0x7F800000, None,
                                  ALU.bitwise_and).then_inc(wscale, 1)
                dve.wait_ge(wscale, done + 2)
                dve.reciprocal(inv_w[:, g], c_w[:, g]).then_inc(wscale, 1)
                dve.wait_ge(wscale, done + 3)
                dve.tensor_scalar(s_w[:, g], inv_w[:, g], WTOP, None, ALU.mult).then_inc(wscale, 1)
                dve.tensor_scalar(c_w[:, g], c_w[:, g], 1.0 / (WTOP * XS), None, ALU.mult).then_inc(wscale, 1)

            def rest_wq(n):
                i, group = WQ_ORDER[n], min(n, 1)
                dve.wait_ge(wscale, 5 * group + 5)
                dve.wait_ge(wq_hi_s, n + 1)
                dve.scalar_tensor_tensor(wq_lo_f[:, i * WQ:(i + 1) * WQ], wq_raw(n),
                                         s_w[:, group:group + 1], wq_hi_f[:, i * WQ:(i + 1) * WQ],
                                         ALU.mult, ALU.subtract).then_inc(wq_lo_s, 1)

            def abs_sum(n):
                (m, g), (src, come, value) = SUMS[n], sum_piece(n)
                dve.wait_ge(come, value)
                dve.tensor_reduce(absum[:, m, g:g + 1], src, AX.X, ALU.add,
                                  apply_absolute_value=True).then_inc(absdve_s, 1)

            def scales():
                dve.wait_ge(absact_s, len(ACT_SUMS))
                dve.wait_ge(absdve_s, len(DVE_SUMS))
                dve.tensor_reduce(absum3[:, :], absum[:, :, :], AX.X, ALU.add).then_inc(absum_s, 1)
                dve.wait_ge(mean3_s, 1)
                dve.tensor_scalar(scale3[:, :], stat[:, 0:3], QUANT_EPS, None, ALU.add).then_inc(absum_s, 1)
                dve.wait_ge(absum_s, 2)
                dve.tensor_scalar(half3[:, :], scale3[:, :], 0.5, None, ALU.mult).then_inc(scales_s, 1)
                dve.tensor_scalar(nhalf3[:, :], scale3[:, :], -0.5, None, ALU.mult).then_inc(scales_s, 1)
                dve.tensor_scalar(c_up[:, :], scale3[:, 0:1], 1.0 / (XS * TERN[0]), None, ALU.mult)\
                    .then_inc(scales_s, 1)
                dve.reciprocal(inv_up[:, 0:1], scale3[:, 0:1]).then_inc(absum_s, 1)
                dve.tensor_tensor(c_ffn[:, 0:1], scale3[:, 0:1], scale3[:, 1:2], ALU.mult).then_inc(absum_s, 1)
                dve.wait_ge(absum_s, 4)
                dve.tensor_scalar(inv_up[:, 1:2], inv_up[:, 0:1], HS, None, ALU.mult).then_inc(scales_s, 1)
                dve.tensor_tensor(c_ffn[:, 1:2], c_ffn[:, 0:1], scale3[:, 2:3], ALU.mult).then_inc(scales_s, 1)
                dve.wait_ge(scales_s, 5)
                dve.tensor_scalar(c_ffn[:, 2:3], c_ffn[:, 1:2], 1.0 / (HS * XS * TERN[1] * TERN[2]), None,
                                  ALU.mult).then_inc(scales_s, 1)
                dve.wait_ge(scales_s, 6)

            def quantise(n):
                g, m = divmod(n, 3)
                cols = slice(g * PIECE, (g + 1) * PIECE)
                if m == 0:
                    if g == 0:
                        piece_in(dve, n)
                        dve.tensor_scalar(below[:, 0, :], stage[:, n % STAGES, :], nhalf3[:, 0:1], None,
                                          ALU.is_lt).then_inc(below0_s, 1)
                        dve.wait_ge(below0_s, 1)
                    else:
                        dve.wait_ge(below_s, g)
                    dve.scalar_tensor_tensor(tern[0][:, cols], stage[:, n % STAGES, :], half3[:, 0:1],
                                             below[:, g % 2, :], ALU.is_gt, ALU.subtract).then_inc(tern_s, 1)
                else:
                    i = 2 * g + m - 1
                    dve.wait_ge(signs_s, i + 1)
                    dve.tensor_tensor(tern[m][:, cols], sign_hi[:, i % 2, :], sign_lo[:, i % 2, :], ALU.add)\
                        .then_inc(tern_s, 1)

            def rest_swi(c, j):
                SB.wait(dve, "swi_hi", c, j + 1)
                SB.wait(dve, "g_mm", c, j - 1)
                dve.tensor_tensor(swi_lo[j % 2][:, :], swi(j % NJ), swi_hi[j % 2][:, :].bitcast(F32),
                                  ALU.subtract).then_inc(SB["swi_lo"], 1)

            def rest_out(c, j):
                SB.wait(dve, "out_hi", c, j + 1)
                SB.wait(dve, "down_done", c, j - 1)
                dve.tensor_tensor(out_lo[:, j % 2, :], w_out(j), out_hi[:, j % 2, :].bitcast(F32),
                                  ALU.subtract).then_inc(SB["out_lo"], 1)

            def rest_y(c, slot):
                SB.wait(dve, "yh_done", c + 1, 1)
                dve.tensor_tensor(yl[slot][:, :, :], yb[:, :, :], yh[slot][:, :, :].bitcast(F32),
                                  ALU.subtract).then_inc(SB["yl_done"], 1)

            def first_y():
                SA.wait(dve, "qkv_mm", LAST, M3)
                rest_y(-1, 0)

            def first_swi():
                rest_swi(0, 0)
                rest_swi(0, 1)

            SA.wait(dve, "stat_mm", 0, 1)
            for k in range(KT):
                dve.tensor_tensor(x[:, k, :], x[:, k, :], stat[:, :], ALU.subtract).then_inc(x0_centred, 1)
            dve.wait_ge(x0_centred, KT)
            dve.sem_inc(SA["centred"], 1)
            dve.sem_inc(SA["stat_read"], 1)
            dve.wait_ge(wq_in[0], 16)
            dve.tensor_reduce(wmax[:, 0:1], wq_raw(0), AX.X, ALU.max, apply_absolute_value=True).then_inc(wmax_s, 1)
            variances(-1)
            scale_wq(0)
            for g in range(PER_T):
                invert_x(-1, g)
            SA.wait(dve, "inv_x", 0, PER_T)

            def norm_tile(k):
                dve.tensor_tensor(x[:, k, :], x[:, k, :], inv2[:, 0, :], ALU.mult).then_inc(x0_norm, 1)

            def low_tile(k):
                dve.wait_ge(x0_norm, k + 1)
                dve.wait_ge(x0_high, k + 1)
                dve.scalar_tensor_tensor(xl[:, 0, k, :], x[:, k, :], XS, xh[:, 0, k, :],
                                         ALU.mult, ALU.subtract).then_inc(x0_low, 1)

            norm_tile(0)
            rest_wq(0)
            norm_tile(1)
            dve.wait_ge(wsum_s, 3)
            dve.tensor_reduce(wmax[:, 1:2], wsum[:, :], AX.X, ALU.max).then_inc(wmax_s, 1)
            norm_tile(2)
            low_tile(0)
            norm_tile(3)
            dve.wait_ge(x0_norm, KT)
            dve.sem_inc(SA["norms"], 1)
            low_tile(1)
            scale_wq(1)
            low_tile(2)
            low_tile(3)
            dve.wait_ge(x0_low, KT)
            dve.sem_inc(SA["xl_done"], 1)
            rest_wq(1)
            first_jobs = {n: [(abs_sum, i)] for n, i in enumerate(DVE_SUMS)}
            first_jobs[1] += [(rest_wq, 2)]
            first_jobs[4] += [(invert_x, -1, PER_T)]
            first_jobs[5] += [(invert_x, -1, g) for g in range(PER_T + 1, 2 * PER_T)]
            first_jobs[6] += [(rms_terms, -1)]
            first_jobs[9] = [(scales,), (quantise, 0)]

            def chunk(c, half):
                def read_qkv(n):
                    group = min(WQ_ORDER.index(QKV_ORDER[n] // 3), 1)
                    undo = c_w[:, group:group + 1]
                    SA.wait(dve, "qkv_mm", c, n + 1)
                    if n < 2 * KT:
                        if n >= KT:
                            SA.wait(dve, "y_done", c, 0)
                        dve.tensor_scalar(kqv[:, n, :], ring[n % 3][:, :], undo, None, ALU.mult)\
                            .then_inc(SA["qkv_read"], 1)
                    else:
                        SA.wait(dve, "y_stored", c, 0)
                        dve.scalar_tensor_tensor(kqv[:, n, :], ring[n % 3][:, :], undo, r_t[:, :],
                                                 ALU.mult, ALU.mult).then_inc(SA["qkv_read"], 1)

                def mean_square(which):
                    SA.wait(dve, "stat_mm", c, 3 + which)
                    dve.scalar_tensor_tensor(kq_ms[:, which, :], m2[:, :], RMS_EPS, stat[:, :],
                                             ALU.mult, ALU.add).then_inc(SA["stat_read"], 1)

                if not is_first(c):
                    SA.wait(dve, "den_done", c, 0)
                for n in range(M3):
                    if is_first(c) and n % 3 == 0:
                        wq_split(dve, n // 3)
                    if n == 2 * KT:
                        SA.wait(dve, "norms", c, 3)
                    read_qkv(n)
                    if n == 2 * KT + 1:
                        mean_square(0)
                    if is_first(c):
                        for job in first_jobs.get(n, []):
                            job[0](*job[1:])
                if is_first(c):
                    for n in QUANT_AT[-1][1:]:
                        quantise(n)
                mean_square(1)

                def invert_kq(g):
                    i, o = g // PER_T, g % PER_T * GRAN
                    SA.wait(dve, "kq_root", c, 1)
                    dve.reciprocal(kq_ms[:, i, o:o + GRAN], kq_ms[:, i, o:o + GRAN]).then_inc(SA["inv_kq"], 1)

                def running_sum(n):
                    which, t = n // KT, n % KT
                    tile = (K0 if which == 0 else V0) + t
                    if which == 0:
                        SA.wait(dve, "wv_done", c, KT)
                    start = carry[:, which, t:t + 1] if half else (DEN_EPS if which == 0 else 0.0)
                    dve.tensor_tensor_scan(kqv[:, tile, :], one_col[:, 0:1].to_broadcast([P, T]),
                                           kqv[:, tile, :], start, ALU.mult, ALU.add)\
                        .then_inc(SA["summed"], 1)

                def keep_ends():
                    SA.wait(dve, "summed", c, 2 * KT)
                    for which, tile in ((0, K0), (1, V0)):
                        dve.tensor_copy(carry[:, which, :], kqv[:, tile:tile + KT, T - 1:T]
                                        .rearrange("p k o -> p (k o)")).then_inc(SA["summed"], 1)

                def denominators():
                    SA.wait(dve, "exped", c, 2)
                    SA.wait(dve, "summed", c, KT)
                    dve.scalar_tensor_tensor(kqv[:, Q0:Q0 + KT, :], kqv[:, Q0:Q0 + KT, :], 1.0,
                                             kqv[:, K0:K0 + KT, :], ALU.add, ALU.mult)\
                        .then_inc(SA["den_done"], 1)

                def invert_den(g):
                    t, o = Q0 + g // PER_T, g % PER_T * GRAN
                    SA.wait(dve, "den_done", c, 1)
                    SA.wait(dve, "summed", c, 2 * KT + 2)
                    dve.reciprocal(kqv[:, t, o:o + GRAN], kqv[:, t, o:o + GRAN]).then_inc(SA["inv_den"], 1)

                jobs = {0: [(invert_kq, 0), (invert_kq, 1)], 1: [(invert_kq, 2), (invert_kq, 3)],
                        7: [(running_sum, 0), (running_sum, 1), (running_sum, 2)],
                        8: [(running_sum, 3), (running_sum, 4), (running_sum, 5)],
                        9: [(running_sum, 6), (running_sum, 7), (keep_ends,)],
                        10: [(denominators,), (invert_den, 0)]}
                if is_last(c):
                    jobs |= {11: [(invert_den, 1), (invert_den, 2)],
                             12: [(invert_den, 3), (first_y,)],
                             13: [(invert_den, 4), (invert_den, 5)],
                             14: [(invert_den, 6), (invert_den, 7)],
                             15: [(first_swi,)]}
                else:
                    jobs |= {3: [(centre, c)],
                             10: [(variances, c)] + jobs[10],
                             11: [(invert_x, c, 0), (invert_x, c, 1)],
                             12: [(invert_x, c, 2), (invert_x, c, 3)],
                             13: [(normalise, c), (rms_terms, c)],
                             14: [(invert_den, 1), (invert_den, 2)],
                             15: [(low_x, c, 1 - half), (invert_den, 3)],
                             16: [(invert_den, 4), (invert_den, 5), (invert_den, 6), (invert_den, 7)]}
                for j in range(NJ + 1):
                    if j < NJ:
                        SA.wait(dve, "s_done", c, j + 1)
                        SA.wait(dve, "g_mm", c, j + 1)
                        SA.wait(dve, "hl_done", c, j - 1)
                        SA.wait(dve, "hh_done", c, j - 1)
                        dve.scalar_tensor_tensor(h[:, j % 2, :], s_act[:, j % 2, :], inv_up[:, 1:2],
                                                 ring[(2 * j + 1) % 3][:, :], ALU.mult, ALU.mult)\
                            .then_inc(SA["h_done"], 1)
                    for job in jobs.get(j, []):
                        job[0](*job[1:])
                    if is_first(c):
                        for n in QUANT_AT.get(j, ()):
                            quantise(n)

            each_chunk(dve, chunk)
            SA.wait(dve, "hh_done", LAST, NJ)
            SA.wait(dve, "hl_done", LAST, NJ)
            SA.wait(dve, "down_done", LAST, NJ)
            SA.wait(dve, "xn_stored", LAST, 16)
            SA.wait(dve, "norms", LAST, 3)

            def attend(c, half):
                for j in range(NJ + 1):
                    if j >= 1 and (j + 1 < NJ or not is_last(c)):
                        rest_swi(c, j + 1)
                    if j < NJ:
                        SB.wait(dve, "s_done", c, j + 1)
                        SB.wait(dve, "g_mm", c, j + 1)
                        SB.wait(dve, "hh_done", c, j - 1)
                        SB.wait(dve, "hl_done", c, j - 1)
                        dve.tensor_tensor(h[:, j % 2, :], s_act[:, j % 2, :], ring[(2 * j + 1) % 4][:, :],
                                          ALU.mult).then_inc(SB["h_done"], 1)
                    if j >= 1:
                        i = j - 1
                        SB.wait(dve, "hh_done", c, i + 1)
                        SB.wait(dve, "down_done", c, i - 2)
                        dve.tensor_tensor(hlb[:, i % 3, :], h[:, i % 2, :], hhb[:, i % 3, :].bitcast(F32),
                                          ALU.subtract).then_inc(SB["hl_done"], 1)
                        rest_out(c, i)
                    if j == 8 and not is_last(c):
                        rest_y(c, 1 - half)
                if not is_last(c):
                    SB.wait(dve, "down_done", c, NJ)
                SB.wait(dve, "base_done", c, 1)
                for t in range(KT):
                    if is_last(c):
                        dve.wait_ge(acc_last, t + 1)
                    dve.tensor_tensor(gb[:, t, :], gb[:, t, :], acc[t][:, :], ALU.mult)\
                        .then_inc(SB["acc_read"], 1)
                    SB.wait(dve, "acc_read", c, t + 1)
                    dve.tensor_tensor(xnb[:, t, :], gb[:, t, :], xb[:, t, :], ALU.add)\
                        .then_inc(SB["out_ready"], 1)

            each_chunk(dve, attend)

        @block.tensor
        def _(pe):
            def mean_over_features(c, k):
                SA.wait(pe, "fold_done", c, 3 * (k - 2))
                SA.wait(pe, "stat_read", c, k - 1)
                pe.matmul(stat[:, :], mean_r[:, :], add_hi[:, :], start=True, stop=False)
                pe.matmul(stat[:, :], mean_r[:, :], add_lo[:, :], start=False, stop=True)\
                    .then_inc(SA["stat_mm"], 1)

            def first_mean(bank, src, tile_ready):
                for k in range(KT):
                    tile_ready(k)
                    last = pe.matmul(bank[:, :], mean_w[:, :], src[:, k, :], start=(k == 0), stop=(k == KT - 1))
                last.then_inc(SA["stat_mm"], 1)

            def mean_of_weights():
                pe.wait_ge(absum_s, 1)
                SA.wait(pe, "stat_read", 0, 3)
                pe.matmul(stat[:, 0:3], count_w[:, :], absum3[:, :], start=True, stop=True).then_inc(mean3_s, 1)

            pe.wait_ge(consts, 4)
            first_mean(stat, x, lambda k: pe.wait_ge(x0_in[k], 16))
            first_mean(stat0, sq, lambda k: pe.wait_ge(x0_squared, k + 1))

            def chunk(c, half):
                if not is_first(c):
                    SA.wait(pe, "xh_done", c, 1)
                    SA.wait(pe, "xl_done", c, 1)
                for n, m in enumerate(QKV_ORDER):
                    if n >= 3:
                        SA.wait(pe, "qkv_read", c, n - 2)
                    elif n == 0:
                        SA.wait(pe, "s_done", c, 0)
                        SA.wait(pe, "h_done", c, 0)
                    if is_first(c):
                        wq_split(pe, WQ_ORDER.index(m // 3))
                    i = 0
                    for k in range(KT):
                        if is_first(c) and n == 0:
                            pe.wait_ge(x0_high, k + 1)
                            pe.wait_ge(x0_low, k + 1)
                        for w, a in ((wq_hi, xh), (wq_hi, xl), (wq_lo, xh)):
                            last = pe.matmul(ring[n % 3][:, :], w[:, m, k, :], a[:, half, k, :],
                                             start=(i == 0), stop=(i == 3 * KT - 1))
                            i += 1
                    last.then_inc(SA["qkv_mm"], 1)
                    if n == 2 * KT + 1:
                        mean_over_features(c, 3)
                    if is_first(c) and n == 2 * KT + 2:
                        mean_of_weights()
                if is_first(c):
                    pe.wait_ge(absum_s, 2)

                def project(w, j, bank, done):
                    for i in range(2 * KT):
                        last = pe.matmul(bank[:, :], w[:, j, i // 2, :], (xh, xl)[i % 2][:, half, i // 2, :],
                                         start=(i == 0), stop=(i == 2 * KT - 1))
                    last.then_inc(SA[done], 1)

                for j in range(NJ + LAG):
                    if j < NJ:
                        for which in range(2):
                            m = 2 * j + which
                            if is_first(c) and j % 2 == 0:
                                pe.wait_ge(tern_s, 3 * (j // 2) + 1 + which)
                            if m < 3:
                                SA.wait(pe, "qkv_read", c, M3 - 2 + m)
                            elif (m - 3) % 2 == 0:
                                SA.wait(pe, "s_done", c, (m - 3) // 2 + 1)
                            else:
                                SA.wait(pe, "h_done", c, (m - 3) // 2 + 1)
                            project((up, gate)[which], j, ring[m % 3], ("u_mm", "g_mm")[which])
                            if m == 0:
                                mean_over_features(c, 4)
                    if j >= LAG:
                        i = j - LAG
                        SA.wait(pe, "hl_done", c, i + 1)
                        if i == 0:
                            SA.wait(pe, "g_act", c, 0)
                        if is_first(c) and i % 2 == 0:
                            pe.wait_ge(tern_s, 3 * (i // 2) + 3)
                        for t in range(KT):
                            pe.matmul(acc[t][:, :], down[:, i, t * P:(t + 1) * P], hh[:, i % 3, :],
                                      start=(i == 0), stop=False)
                            last = pe.matmul(acc[t][:, :], down[:, i, t * P:(t + 1) * P], hl[:, i % 3, :],
                                             start=False, stop=(i == NJ - 1))
                        last.then_inc(SA["down_done"], 1)
                    if not is_last(c):
                        if j == 2:
                            mean_over_features(c, 5)
                        if j == 9:
                            mean_over_features(c, 6)

            each_chunk(pe, chunk)
            SA.wait(pe, "s_done", LAST, NJ)
            SA.wait(pe, "h_done", LAST, NJ)
            SA.wait(pe, "stat_read", LAST, 4)

            def attend(c, half):
                SB.wait(pe, "yh_done", c, 1)
                SB.wait(pe, "yl_done", c, 1)
                for j in range(NJ + LAG):
                    if j < NJ:
                        SB.wait(pe, "swi_hi", c, j + 1)
                        SB.wait(pe, "swi_lo", c, j + 1)
                        for which in range(2):
                            SB.wait(pe, ("s_done", "h_done")[which], c, j - 1)
                            i = 0
                            for k in range(KT):
                                col = ((1 - which) * KT + k) * P
                                for w, a in ((swi_hi, yh), (swi_hi, yl), (swi_lo, yh)):
                                    last = pe.matmul(ring[(2 * j + which) % 4][:, :], w[j % 2][:, col:col + P],
                                                     a[half][:, k, :], start=(i == 0), stop=(i == 3 * KT - 1))
                                    i += 1
                            last.then_inc(SB[("u_mm", "g_mm")[which]], 1)
                    if j >= LAG:
                        i = j - LAG
                        SB.wait(pe, "hl_done", c, i + 1)
                        SB.wait(pe, "out_lo", c, i + 1)
                        if i == 0:
                            if is_first(c):
                                SA.wait(pe, "g_act", LAST, KT)
                            else:
                                SB.wait(pe, "acc_read", c, 0)
                        for t in range(KT):
                            n = 0
                            for w, a in ((out_hi, hhb), (out_hi, hlb), (out_lo, hhb)):
                                last = pe.matmul(acc[t][:, :], w[:, i % 2, t * P:(t + 1) * P], a[:, i % 3, :],
                                                 start=(i == 0 and n == 0), stop=(i == NJ - 1 and n == 2))
                                n += 1
                            if is_last(c) and i == NJ - 1:
                                last.then_inc(acc_last, 1)
                        if not (is_last(c) and i == NJ - 1):
                            last.then_inc(SB["down_done"], 1)

            each_chunk(pe, attend)


def kernel(**inputs):
    import numpy as np
    import concourse.bacc as bacc
    from concourse.bass_utils import run_bass_kernel_spmd as run

    def a(name):
        return np.ascontiguousarray(inputs[name])

    def lay(v):
        return np.ascontiguousarray(v)

    x = lay(a("L0_attn_x").reshape(CHUNKS, T, KT, P).transpose(0, 3, 2, 1))
    wqkv = lay(a("L0_attn_w_qkv").reshape(4, 3, P, KT, P).transpose(0, 4, 1, 3, 2)).reshape(4, P, 3 * KT * P)
    wswi = lay(a("L0_attn_w_swiglu").reshape(2, NJ, P, KT, P).transpose(1, 4, 0, 3, 2)).reshape(NJ, P, 2 * KT * P)
    wout = lay(a("L0_attn_w_out").reshape(D, NJ, P).transpose(1, 2, 0))
    up, gate = (lay(a(n).reshape(NJ // 2, 2, P, KT, P).transpose(0, 4, 1, 3, 2)).reshape(NJ // 2, P, 2 * KT * P)
                for n in ("L0_ffn_W_up", "L0_ffn_W_gate"))
    down = lay(a("L0_ffn_W_down").reshape(D, NJ // 2, 2, P).transpose(1, 3, 2, 0)).reshape(NJ // 2, P, 2 * D)

    nc = bacc.Bacc("TRN2", target_bir_lowering=False, num_devices=1)
    arrays = {"x": x, "wqkv": wqkv, "wswi": wswi, "wout": wout, "up": up, "gate": gate, "down": down}
    args = [nc.dram_tensor("in_" + n, v.shape, F32, kind="ExternalInput").ap() for n, v in arrays.items()]
    out = nc.dram_tensor("out_x", (CHUNKS, P, KT, T), F32, kind="ExternalOutput").ap()
    build(nc, *args, out)
    r = run(nc, [{"in_" + n: v for n, v in arrays.items()}], core_ids=[0])
    got = r.results[0]["out_x"]
    return lay(got.transpose(0, 3, 2, 1)).reshape(B, S, D)
```
